# Optimizing a Trainium2 kernel written in Bass

```python
import numpy as np
import jax
import jax.numpy as jnp

def _softmax(x, axis=-1):
    return jax.nn.softmax(x, axis=axis)
def _gelu(x):
    return jax.nn.gelu(x, approximate=True)
def _silu(x):
    return jax.nn.silu(x)
def _sigmoid(x):
    return jax.nn.sigmoid(x)
def _layernorm(x, axis=-1, eps=1e-5):
    m = jnp.mean(x, axis=axis, keepdims=True)
    v = jnp.var(x, axis=axis, keepdims=True)
    return (x - m) / jnp.sqrt(v + eps)
def _scatter_add(tgt, idx, src, axis=0):
    return tgt.at[idx].add(src)
def _segment_sum(src, seg, n):
    return jax.ops.segment_sum(src, seg, n)

kernel_name = 'mk_vit_tower_d1_tok_img256_94b556'

def setup_inputs(seed: int = 0):
    np.random.seed(seed)
    _w = jnp.asarray
    def _rec_inputs():
        import jax
        import jax.numpy as jnp
        _rk = jax.random.key(seed)
        x = (-4.65018e-05 + 0.999886 * jax.random.normal(jax.random.fold_in(_rk, 1), (8, 3, 512, 512), jnp.float32))
        return x
    x = _rec_inputs()
    def _L0_tok_setup():
        import jax, jax.numpy as jnp
        import numpy as np
        B, C, H, P, D = (64, 3, 512, 16, 256)
        NP = H // P
        key = jax.random.key(seed)
        ks = jax.random.split(key, 7)
        s = lambda fan_in: 1.0 / np.sqrt(fan_in)
        return {'x': jax.random.normal(ks[0], (B, C, H, H), dtype=jnp.float32), 'Wp': jax.random.normal(ks[1], (P * P * C, D), dtype=jnp.float32) * s(P * P * C), 'bp': jax.random.normal(ks[2], (D,), dtype=jnp.float32) * 0.01, 'W1': jax.random.normal(ks[3], (2, D), dtype=jnp.float32) * s(2), 'b1': jax.random.normal(ks[4], (D,), dtype=jnp.float32) * 0.01, 'W2': jax.random.normal(ks[5], (D, D), dtype=jnp.float32) * s(D), 'b2': jax.random.normal(ks[6], (D,), dtype=jnp.float32) * 0.01}
    _L0_tok_all = _L0_tok_setup()
    _L0_tok_in = {k: v for k, v in _L0_tok_all.items() if k in ('Wp', 'bp', 'W1', 'b1', 'W2', 'b2', )}
    del _L0_tok_all

    def _L0_attn_setup():
        import jax, jax.numpy as jnp
        import numpy as np
        H, D = (8, 32)
        EPS = 1e-05
        key = jax.random.key(seed)
        ks = jax.random.split(key, 4)
        B, N, C = (2, 2048, 256)
        inner = H * D
        return {'node_features': jax.random.normal(ks[0], (B, N, C), jnp.float32), 'ln_gamma': jnp.ones((C,), jnp.float32), 'ln_beta': jnp.zeros((C,), jnp.float32), 'W_qkv': jax.random.normal(ks[1], (3 * inner, C), jnp.float32) * 0.02, 'W_gate': jax.random.normal(ks[2], (inner, C), jnp.float32) * 0.02, 'b_gate': jnp.ones((inner,), jnp.float32), 'W_final': jax.random.normal(ks[3], (C, inner), jnp.float32) * 0.02, 'b_final': jnp.zeros((C,), jnp.float32)}
    _L0_attn_all = _L0_attn_setup()
    _L0_attn_in = {k: v for k, v in _L0_attn_all.items() if k in ('ln_gamma', 'ln_beta', 'W_qkv', 'W_gate', 'b_gate', 'W_final', 'b_final', )}
    del _L0_attn_all

    def _L0_ffn_setup():
        import jax, jax.numpy as jnp
        import numpy as np
        C = 256
        HID = 1024
        E = 8
        TEMP = 1.0
        key = jax.random.key(seed)
        ks = jax.random.split(key, 7)
        x = jax.random.normal(ks[0], (8, 16384, C), dtype=jnp.float32)
        W1 = jax.random.normal(ks[1], (C, HID), dtype=jnp.float32) * 0.02
        b1 = jnp.zeros((HID,), dtype=jnp.float32)
        Wg = jax.random.normal(ks[2], (HID, E), dtype=jnp.float32) * 0.02
        bg = jnp.zeros((E,), dtype=jnp.float32)
        Wd = jax.random.normal(ks[3], (E, HID, C), dtype=jnp.float32) * 0.02
        bd = jnp.zeros((E, C), dtype=jnp.float32)
        return {'x': x, 'W1': W1, 'b1': b1, 'Wg': Wg, 'bg': bg, 'Wd': Wd, 'bd': bd}
    _L0_ffn_all = _L0_ffn_setup()
    _L0_ffn_in = {k: v for k, v in _L0_ffn_all.items() if k in ('W1', 'b1', 'Wg', 'bg', 'Wd', 'bd', )}
    del _L0_ffn_all

    return {
        "x": x,
        "L0_tok_Wp": _L0_tok_in["Wp"],
        "L0_tok_bp": _L0_tok_in["bp"],
        "L0_tok_W1": _L0_tok_in["W1"],
        "L0_tok_b1": _L0_tok_in["b1"],
        "L0_tok_W2": _L0_tok_in["W2"],
        "L0_tok_b2": _L0_tok_in["b2"],
        "L0_attn_ln_gamma": _L0_attn_in["ln_gamma"],
        "L0_attn_ln_beta": _L0_attn_in["ln_beta"],
        "L0_attn_W_qkv": _L0_attn_in["W_qkv"],
        "L0_attn_W_gate": _L0_attn_in["W_gate"],
        "L0_attn_b_gate": _L0_attn_in["b_gate"],
        "L0_attn_W_final": _L0_attn_in["W_final"],
        "L0_attn_b_final": _L0_attn_in["b_final"],
        "L0_ffn_W1": _L0_ffn_in["W1"],
        "L0_ffn_b1": _L0_ffn_in["b1"],
        "L0_ffn_Wg": _L0_ffn_in["Wg"],
        "L0_ffn_bg": _L0_ffn_in["bg"],
        "L0_ffn_Wd": _L0_ffn_in["Wd"],
        "L0_ffn_bd": _L0_ffn_in["bd"],
    }

def reference(x, L0_tok_Wp, L0_tok_bp, L0_tok_W1, L0_tok_b1, L0_tok_W2, L0_tok_b2, L0_attn_ln_gamma, L0_attn_ln_beta, L0_attn_W_qkv, L0_attn_W_gate, L0_attn_b_gate, L0_attn_W_final, L0_attn_b_final, L0_ffn_W1, L0_ffn_b1, L0_ffn_Wg, L0_ffn_bg, L0_ffn_Wd, L0_ffn_bd):
    import jax
    import jax.numpy as jnp
    def _L0_tok_ref(x, Wp, bp, W1, b1, W2, b2):
        import jax, jax.numpy as jnp
        import numpy as np
        B, C, H, P, D = (64, 3, 512, 16, 256)
        NP = H // P
        b = x.shape[0]
        patches = x.reshape(b, C, NP, P, NP, P)
        patches = patches.transpose(0, 2, 4, 1, 3, 5).reshape(b, NP * NP, C * P * P)
        embedded = jnp.einsum('bnk,kd->bnd', patches, Wp) + bp
        gx, gy = jnp.meshgrid(jnp.arange(NP, dtype=jnp.float32), jnp.arange(NP, dtype=jnp.float32), indexing='ij')
        xy = jnp.stack([gx, gy], axis=-1).reshape(1, -1, 2) / (NP - 1)
        pos = jax.nn.relu(xy @ W1 + b1) @ W2 + b2
        return embedded + pos

    def _L0_attn_ref(node_features, ln_gamma, ln_beta, W_qkv, W_gate, b_gate, W_final, b_final):
        import jax, jax.numpy as jnp
        import numpy as np
        H, D = (8, 32)
        EPS = 1e-05
        x = node_features
        B, N, _ = x.shape
        mu = jnp.mean(x, axis=-1, keepdims=True)
        var = jnp.mean(jnp.square(x - mu), axis=-1, keepdims=True)
        normed = (x - mu) / jnp.sqrt(var + EPS) * ln_gamma + ln_beta
        qkv = normed @ W_qkv.T
        q, k, v = jnp.split(qkv, 3, axis=-1)

        def to_heads(t):
            return t.reshape(B, N, H, D).transpose(0, 2, 1, 3)
        q, k, v = (to_heads(q), to_heads(k), to_heads(v))
        gate = jax.nn.sigmoid(to_heads(x @ W_gate.T + b_gate))
        scores = jnp.einsum('bhid,bhjd->bhij', q, k) * D ** (-0.5)
        attn = jax.nn.softmax(scores, axis=-1)
        out = jnp.einsum('bhij,bhid->bhjd', attn, v) * gate
        out = out.transpose(0, 2, 1, 3).reshape(B, N, H * D)
        return x + out @ W_final.T + b_final

    def _L0_ffn_ref(x, W1, b1, Wg, bg, Wd, bd):
        import jax, jax.numpy as jnp
        import numpy as np
        C = 256
        HID = 1024
        E = 8
        TEMP = 1.0
        orig_shape = x.shape
        xf = x.reshape(-1, orig_shape[-1])
        H = jax.nn.gelu(xf @ W1 + b1, approximate=False)
        probs = jax.nn.softmax((H @ Wg + bg) / TEMP, axis=-1)
        assign = jnp.argmax(probs, axis=-1)
        out = jnp.zeros_like(xf)
        for e in range(Wd.shape[0]):
            y = H @ Wd[e] + bd[e]
            sel = (assign == e)[:, None]
            out = out + jnp.where(sel, probs[:, e:e + 1] * y, 0.0)
        return out.reshape(orig_shape)

    h = _L0_tok_ref(x, L0_tok_Wp, L0_tok_bp, L0_tok_W1, L0_tok_b1, L0_tok_W2, L0_tok_b2)
    h = h + _L0_attn_ref(_layernorm(h, axis=-1), L0_attn_ln_gamma, L0_attn_ln_beta, L0_attn_W_qkv, L0_attn_W_gate, L0_attn_b_gate, L0_attn_W_final, L0_attn_b_final)
    h = h + _L0_ffn_ref(_layernorm(h, axis=-1), L0_ffn_W1, L0_ffn_b1, L0_ffn_Wg, L0_ffn_bg, L0_ffn_Wd, L0_ffn_bd)
    return h


_drawn_inputs = setup_inputs


def setup_inputs(seed=0):
    import zlib

    import numpy as np

    out = dict(_drawn_inputs(seed))
    spreads = {'L0_attn_ln_gamma': (1.0, 0.6),
     'L0_attn_ln_beta': (0.0, 0.8),
     'L0_attn_b_gate': (1.0, 0.6),
     'L0_attn_b_final': (0.0, 0.1),
     'L0_ffn_b1': (0.0, 0.8),
     'L0_ffn_bg': (0.0, 0.779),
     'L0_ffn_bd': (0.0, 0.8)}
    factors = {'L0_tok_bp': 5.893,
     'L0_tok_b1': 8.0,
     'L0_tok_b2': 5.771,
     'L0_attn_W_qkv': 4.428,
     'L0_attn_W_gate': 8.0,
     'L0_attn_W_final': 4.429,
     'L0_ffn_W1': 5.391,
     'L0_ffn_Wg': 5.849,
     'L0_ffn_Wd': 6.698}
    for name, (base, spread) in spreads.items():
        noise = np.random.default_rng([zlib.crc32(name.encode()), seed]).standard_normal(out[name].shape)
        drawn = base * np.exp(spread * noise) if base else spread * noise
        out[name] = jnp.asarray(drawn.astype(out[name].dtype))
    for name, factor in factors.items():
        out[name] = (out[name] * factor).astype(out[name].dtype)
    return out
```

```python
from contextlib import ExitStack

import concourse.bass as bass
from concourse import mybir

F32 = mybir.dt.float32
F32R = mybir.dt.float32r
I32 = mybir.dt.int32
ALU = mybir.AluOpType
ACT = mybir.ActivationFunctionType
AX_X = mybir.AxisListType.X

P = 128
IMAGES = 8
TOKENS = 1024
TILES = TOKENS // P
ALL_TILES = IMAGES * TILES
D = 256
DC = D // P
KC = 3 * 16 * 16 // P
HALF = TOKENS // 2
HEADS, HD = 8, 32
GROUPS = HEADS // 4
STEPS = HEADS * TILES
HID = 1024
HC = HID // P
EXPERTS = 8
SLOTS = ALL_TILES + EXPERTS
GROUP = 4
SORT_GROUPS = SLOTS // GROUP
QUARTER = TOKENS // 4
PR = 6
SR = 3
EPS = 1e-5
SCALE = float(HD) ** -0.5


def vit_layer_kernel(nc, x, w_patch, pos_in, pos_w1, pos_w2, pos_bias, ln_gamma, ln_beta, w_qk, w_v,
                     w_gate, b_gate, w_final, b_final, w_ffn1, b_ffn1, w_router, b_router, w_down,
                     b_down, identity, upper, rank, slot_start, token_id, out):
    xn_rows = nc.dram_tensor("xn_rows", (ALL_TILES * P, D), F32).ap()
    h_rows = nc.dram_tensor("h_rows", (ALL_TILES * P, D), F32).ap()
    y_rows = nc.dram_tensor("y_rows", (SLOTS * P, D), F32).ap()
    sorted_ids = nc.dram_tensor("sorted_ids", (SLOTS * P, 1), I32).ap()

    h_view = h_rows.rearrange("(b t p) d -> b p t d", b=IMAGES, t=TILES)
    xn_view = xn_rows.rearrange("(b t p) d -> b p t d", b=IMAGES, t=TILES)
    y_view = y_rows.rearrange("(g t p) d -> g p t d", t=GROUP, p=P)
    out_view = out.rearrange("b (t p) d -> b p t d", p=P)

    with ExitStack() as ctx:
        def sem(name):
            return ctx.enter_context(nc.semaphore(name))

        def tensor(stack, name, shape, dt=F32):
            return stack.enter_context(nc.sbuf_tensor(name, shape, dt))

        ps = ctx.enter_context(nc.psum_tensor("ps", [P, 8, 512], F32))

        ident = tensor(ctx, "ident", [P, P])
        wf1 = tensor(ctx, "wf1", [P, DC, HID])
        bf1 = tensor(ctx, "bf1", [P, HC])
        ones = tensor(ctx, "ones", [P, P])
        logits = tensor(ctx, "logits", [P, ALL_TILES, EXPERTS])
        prob = tensor(ctx, "prob", [P, ALL_TILES])
        place_i = tensor(ctx, "place_i", [P, ALL_TILES], I32)
        slot_expert = tensor(ctx, "slot_expert", [P, SLOTS], I32)

        sa = ExitStack()
        wp = tensor(sa, "wp", [P, KC, D])
        wqk = tensor(sa, "wqk", [P, DC, 2 * D])
        wv = tensor(sa, "wv", [P, DC, D])
        wg = tensor(sa, "wg", [P, DC, D])
        wfin = tensor(sa, "wfin", [P, DC, D])
        wr = tensor(sa, "wr", [P, HC, 32])
        posb = tensor(sa, "posb", [P, TILES, D])
        vecs = tensor(sa, "vecs", [P, 3, DC])
        gamma, beta, bgate = vecs[:, 0, :], vecs[:, 1, :], vecs[:, 2, :]
        nbgate = tensor(sa, "nbgate", [P, DC])
        bfin = tensor(sa, "bfin", [P, D])
        pick = tensor(sa, "pick", [P, EXPERTS])
        xt = tensor(sa, "xt", [P, 2, KC, QUARTER])
        h = tensor(sa, "h", [P, TILES, D])
        a = tensor(sa, "a", [P, TILES, D])
        n = tensor(sa, "n", [P, TILES, D])
        nt = tensor(sa, "nt", [P, DC, TOKENS])
        at = tensor(sa, "at", [P, DC, TOKENS])
        qk = tensor(sa, "qk", [P, 2, 2, TOKENS], F32R)
        stq = tensor(sa, "stq", [96, HEADS, TOKENS], F32R)
        stk = tensor(sa, "stk", [96, HEADS, TOKENS], F32R)
        v = tensor(sa, "v", [P, TILES, D])
        vs = tensor(sa, "vs", [P, 2, 4, HD])
        pr = tensor(sa, "pr", [P, PR, TOKENS])
        lt = tensor(sa, "lt", [P, HALF])
        bst = tensor(sa, "bst", [P, TILES, 6])
        mv = tensor(sa, "mv", [P, TILES, 2])
        rstd = tensor(sa, "rstd", [P, TILES])
        half_neg = tensor(sa, "half_neg", [P, TILES])
        vare = tensor(sa, "vare", [P, TILES])
        nmax = tensor(sa, "nmax", [P, 16])
        rsum = tensor(sa, "rsum", [P, 16])
        rinv = tensor(sa, "rinv", [P, 2, 4])
        gate = a[:].rearrange("p t d -> p (t d)").rearrange("p (c n) -> p c n", c=DC)
        og = n[:].rearrange("p t d -> p (t d)").rearrange("p (c n) -> p c n", c=DC)
        h_flat = h[:].rearrange("p t d -> p (t d)")
        ht = [qk[:].bitcast(F32).rearrange("p a b n -> p (a b n)").rearrange("p (k n) -> p k n", k=HC),
              pr[:].rearrange("p r n -> p (r n)")[:, 0:HC * HALF].rearrange("p (k n) -> p k n", k=HC)]
        posin = pr[0:3, 0, :]
        posw1 = pr[0:3, 1, 0:D]
        sa.close()

        sc = ExitStack()
        wd = tensor(sc, "wd", [P, EXPERTS, HC, D])
        bd = tensor(sc, "bd", [1, EXPERTS, D])
        up = tensor(sc, "up", [P, P])
        rnk = tensor(sc, "rnk", [P, ALL_TILES, EXPERTS])
        brt = tensor(sc, "brt", [P, ALL_TILES, EXPERTS])
        sst = tensor(sc, "sst", [P, SLOTS])
        tid = tensor(sc, "tid", [P, ALL_TILES], I32)
        ee = tensor(sc, "ee", [P, ALL_TILES, EXPERTS])
        oh = tensor(sc, "oh", [P, ALL_TILES, EXPERTS])
        tot = tensor(sc, "tot", [P, ALL_TILES, EXPERTS])
        run = tensor(sc, "run", [P, ALL_TILES, EXPERTS])
        red = tensor(sc, "red", [P, 4, ALL_TILES])
        onesf = tensor(sc, "onesf", [P, ALL_TILES])
        cnt_i = tensor(sc, "cnt_i", [P, 2, EXPERTS], I32)
        cnt = tensor(sc, "cnt", [P, 3, EXPERTS])
        slot_f = tensor(sc, "slot_f", [P, 2, SLOTS])
        place_f = tensor(sc, "place_f", [P, ALL_TILES])
        place_a = tensor(sc, "place_a", [P, 3, ALL_TILES], I32)
        inv_pos = tensor(sc, "inv_pos", [P, 2, 8], I32)
        inv_tok = tensor(sc, "inv_tok", [P, 2, 8], I32)
        inv = tensor(sc, "inv", [P, SLOTS], I32)
        idx = tensor(sc, "idx", [P, 2, GROUP], I32)
        xg = tensor(sc, "xg", [P, 2, GROUP, D])
        xgt = tensor(sc, "xgt", [P, 2, DC, 512])
        hg = tensor(sc, "hg", [P, 2, HC, 512])
        yo = tensor(sc, "yo", [P, 2, GROUP, D])
        back = tensor(sc, "back", [P, 2, 8], I32)
        pcol = tensor(sc, "pcol", [P, 2, 8])
        yg = tensor(sc, "yg", [P, 2, 8, D])
        hr = tensor(sc, "hr", [P, 2, 8, D])
        sc.close()

        s = {}
        for name in ("consts", "setup", "pos_mm", "pos_relu", "pos_mm2", "pos_done", "vec_chain",
                     "x_in0", "x_in1", "emb_mm", "emb_h", "var_ready", "rstd_ready", "a_ready",
                     "n_ready", "tr_mm", "nt_ready", "at_ready", "ha_ready", "pool_chain", "qk_mm",
                     "qk_hi", "qk_lo", "v_mm", "v_ready", "g_mm", "g_exp", "g_one", "g_ready",
                     "stack0", "stack1", "score_mm", "max_done", "exp_done", "vs_ready", "pv_mm",
                     "og_ready", "fin_mm", "fin_h", "h_out", "xn_ready", "xn_out", "xt_mm",
                     "xt_ready", "ff_mm", "ff_act", "lg_mm", "lt_ready", "lg2_mm", "lg_done",
                     "ids_zero", "c_consts", "wd_in", "r_exp", "r_oh", "r_mm", "place_ready",
                     "slots_ready", "inv_stage", "inv_out0", "inv_out1", "inv_in", "idx_ready",
                     "xg_in0", "xg_in1", "gt_mm", "gt_ready", "gf_mm", "gf_act", "y_mm", "y_ready",
                     "y_out0", "y_out1", "back_idx", "yg_in0", "yg_in1", "hr_in0", "hr_in1", "o_ready",
                     "o_out0", "o_out1", "pcol_ready"):
            s[name] = sem(name)
        S = s
        x_in = [s["x_in0"], s["x_in1"]]
        stack = [s["stack0"], s["stack1"]]
        posr = nt
        posw2 = at[:, 0, 0:DC * D].rearrange("p (c d) -> p c d", c=DC)
        posbias = at[0:2, 1, 0:D]
        N_CONST = 19

        def hold(eng, semaphore, value):
            value = eng.to_reg(value)
            eng.wait_ge(S["setup"], 1)
            eng.wait_ge(semaphore, value)

        block = ctx.enter_context(nc.Block())

        @block.sync
        def _(sp):
            for dst, src in ((posin, pos_in), (posw1, pos_w1), (posw2, pos_w2), (posbias, pos_bias),
                             (wp[:], w_patch), (ident[:], identity), (vecs[:, 0, :], ln_gamma),
                             (vecs[:, 1, :], ln_beta), (vecs[:, 2, :], b_gate), (wqk[:], w_qk), (wv[:], w_v),
                             (wg[:], w_gate), (wfin[:], w_final), (bfin[:], b_final), (wf1[:], w_ffn1),
                             (bf1[:], b_ffn1), (wr[:], w_router), (pick[:], rank[:, 0, EXPERTS:])):
                sp.dma_start(dst, src).then_inc(S["consts"], 16)
            sp.dma_start(sorted_ids.rearrange("(p q) o -> p (q o)", p=P), token_id[:, ALL_TILES:]
                         ).then_inc(S["ids_zero"], 16)
            for q in range(2):
                sp.dma_start(xt[:, q], x[0, q]).then_inc(x_in[q], 16)
            with sp.Fori(0, IMAGES) as b:
                for q in (2, 3):
                    hold(sp, S["emb_mm"], b * TILES + 2 * (q - 1))
                    sp.dma_start(xt[:, q % 2], x[b, q]).then_inc(x_in[q % 2], 16)
                for g in range(GROUPS):
                    hold(sp, S["qk_lo"], b * 8 + 4 * (g + 1))
                    if g == 0:
                        hold(sp, S["score_mm"], b * STEPS)
                    for hh in range(4):
                        for r in range(3):
                            src = slice(32 * hh, 32 * hh + 32)
                            dst = slice(32 * r, 32 * r + 32)
                            sp.dma_start(stq[dst, 4 * g + hh, :].bitcast(F32), qk[src, 0, r % 2, :].bitcast(F32)).then_inc(stack[g], 16)
                            sp.dma_start(stk[dst, 4 * g + hh, :].bitcast(F32), qk[src, 1, r // 2, :].bitcast(F32)).then_inc(stack[g], 16)
                    if g == 0:
                        for q in range(2):
                            hold(sp, S["emb_mm"], b * TILES + 2 * (q + 3))
                            sp.dma_start(xt[:, q], x[b + 1, q]).then_inc(x_in[q], 16)
                hold(sp, S["fin_h"], b * 4 + 4)
                sp.dma_start(h_view[b], h[:]).then_inc(S["h_out"], 16)
                hold(sp, S["xn_ready"], b * TILES + TILES)
                sp.dma_start(xn_view[b], n[:]).then_inc(S["xn_out"], 16)
            sp.wait_ge(S["lg_done"], 2 * IMAGES)
            sp.wait_ge(S["h_out"], 16 * IMAGES)
            sp.wait_ge(S["xn_out"], 16 * IMAGES)
            for q in range(2):
                sp.wait_ge(x_in[q], 16 * (2 * IMAGES + 1))
            for dst, src in ((up[:], upper), (rnk[:], rank[:, :, 0:EXPERTS]), (brt[:], b_router),
                             (sst[:], slot_start), (tid[:], token_id[:, 0:ALL_TILES]), (bd[:], b_down)):
                sp.dma_start(dst, src).then_inc(S["c_consts"], 16)
            for e in range(EXPERTS):
                sp.dma_start(wd[:, e], w_down[e]).then_inc(S["wd_in"], 16)
            for i in range(2):
                sp.wait_ge([S["inv_out0"], S["inv_out1"]][i], 16 * 8 * (ALL_TILES // 16))
            sp.dma_start(inv[:], sorted_ids.rearrange("(p q) o -> p (q o)", p=P)).then_inc(S["inv_in"], 16)
            with sp.Fori(0, SORT_GROUPS // 2) as g2:
                for i in range(2):
                    hold(sp, S["y_ready"], g2 * 4 + 2 * (i + 1))
                    sp.dma_start(y_view[g2 * 2 + i], yo[:, i]).then_inc([S["y_out0"], S["y_out1"]][i], 16)
            with sp.Fori(0, IMAGES // 2) as j2:
                for i in range(2):
                    hold(sp, S["o_ready"], j2 * 2 + i)
                    sp.dma_start(hr[:, i], h_view[j2 * 2 + i]).then_inc([S["hr_in0"], S["hr_in1"]][i], 16)
                    hold(sp, S["o_ready"], j2 * 2 + i + 1)
                    sp.dma_start(out_view[j2 * 2 + i], yg[:, i]).then_inc([S["o_out0"], S["o_out1"]][i], 16)
            for i in range(2):
                sp.wait_ge([S["o_out0"], S["o_out1"]][i], 16 * (IMAGES // 2))
                sp.wait_ge([S["y_out0"], S["y_out1"]][i], 16 * (SORT_GROUPS // 2))

        @block.gpsimd
        def _(pool):
            chain = [0]

            def link(ins, base=0):
                chain[0] += 1
                ins.then_inc(S["pool_chain"], 1)
                hold(pool, S["pool_chain"], base + chain[0])

            link(nc.gpsimd.memset(half_neg[:], -0.5))
            before = chain[0]
            with pool.Fori(0, IMAGES) as b:
                chain[0] = before
                for ln in range(3):
                    hold(pool, S["var_ready"], b * 3 + ln + 1)
                    link(nc.gpsimd.tensor_scalar(vare[:], mv[:, :, 1], EPS, None, ALU.add), b * 4)
                    nc.gpsimd.tensor_tensor(rstd[:], vare[:], half_neg[:], ALU.pow).then_inc(S["rstd_ready"], 1)
                    if ln == 1:
                        hold(pool, S["n_ready"], b * TILES + TILES)
                        hold(pool, S["tr_mm"], b * 8 + 8)
                        link(nc.gpsimd.tensor_tensor(h[:], h[:], a[:], ALU.add), b * 4)
                        nc.gpsimd.tensor_tensor(h[:], h[:], bfin[:, None, :].broadcast_to([P, TILES, D]), ALU.add).then_inc(S["ha_ready"], 1)
                        for c in range(DC):
                            for hf in range(2):
                                piece = gate[:, c, hf * HALF:(hf + 1) * HALF]
                                hold(pool, S["g_exp"], b * 4 + 2 * c + hf + 1)
                                nc.gpsimd.tensor_scalar(piece, piece, 1.0, None, ALU.add).then_inc(S["g_one"], 1)
            assert chain[0] - before == 4
            pool.wait_ge(S["ids_zero"], 16)
            with pool.Fori(0, ALL_TILES // 16) as j2:
                for i in range(2):
                    hold(pool, S["inv_stage"], j2 * 2 + i + 1)
                    for k in range(8):
                        nc.gpsimd.indirect_dma_start(
                            sorted_ids, bass.IndirectOffsetOnAxis(inv_pos[:, i, k:k + 1], 0),
                            inv_tok[:, i, k:k + 1], None).then_inc([S["inv_out0"], S["inv_out1"]][i], 16)
            pool.wait_ge(S["inv_in"], 16)
            with pool.Fori(0, SORT_GROUPS // 2) as g2:
                for i in range(2):
                    hold(pool, S["gt_mm"], g2 * 4 + 2 * i)
                    nc.gpsimd.tensor_copy(idx[:, i], inv[:, bass.ds(g2 * (2 * GROUP) + i * GROUP, GROUP)]).then_inc(S["idx_ready"], 1)
                    hold(pool, S["idx_ready"], g2 * 2 + i + 1)
                    for t in range(GROUP):
                        nc.gpsimd.indirect_dma_start(
                            xg[:, i, t, :], None, xn_rows,
                            bass.IndirectOffsetOnAxis(idx[:, i, t:t + 1], 0)).then_inc([S["xg_in0"], S["xg_in1"]][i], 16)
            for i in range(2):
                pool.wait_ge([S["y_out0"], S["y_out1"]][i], 16 * (SORT_GROUPS // 2))
            with pool.Fori(0, IMAGES // 2) as j2:
                for i in range(2):
                    hold(pool, [S["o_out0"], S["o_out1"]][i], j2 * 16)
                    nc.gpsimd.tensor_copy(back[:, i], place_i[:, bass.ds(j2 * 16 + 8 * i, 8)]).then_inc(S["back_idx"], 1)
                    hold(pool, S["back_idx"], j2 * 2 + i + 1)
                    for k in range(8):
                        nc.gpsimd.indirect_dma_start(
                            yg[:, i, k, :], None, y_rows,
                            bass.IndirectOffsetOnAxis(back[:, i, k:k + 1], 0)).then_inc([S["yg_in0"], S["yg_in1"]][i], 16)

        @block.tensor
        def _(pe):
            mm = nc.tensor.matmul
            pe.wait_ge(S["consts"], 16 * 18)
            for c in range(DC):
                for hf in range(2):
                    mm(ps[:, 2 * c + hf, :], posw1[:, c * P:(c + 1) * P], posin[:, hf * HALF:(hf + 1) * HALF],
                       start=True, stop=True).then_inc(S["pos_mm"], 1)
            pe.wait_ge(S["pos_relu"], 4)
            pe.wait_ge(S["setup"], 1)
            for t in range(TILES):
                o = ps[:, 4 + t // 2, (t % 2) * D:(t % 2 + 1) * D]
                for c in range(DC):
                    mm(o, posr[:, c, t * P:(t + 1) * P], posw2[:, c, :], start=(c == 0), stop=False, skip_group_check=True)
                mm(o, ones[0:2, :], posbias, start=False, stop=True, skip_group_check=True).then_inc(S["pos_mm2"], 1)
            pe.wait_ge(S["pos_done"], 4)

            with pe.Fori(0, IMAGES) as b:
                pe.wait_ge(S["lg_done"], b * 2)
                for t in range(TILES):
                    if t % 2 == 0:
                        q = t // 2
                        pe.wait_ge(x_in[q % 2], b * 32 + 16 * (q // 2 + 1))
                    for k in range(KC):
                        last = mm(ps[:, t, 0:D], xt[:, q % 2, k, (t % 2) * P:(t % 2 + 1) * P], wp[:, k, :],
                                  start=(k == 0), stop=(k == KC - 1))
                    last.then_inc(S["emb_mm"], 1)
                for hf in range(2):
                    for w in range(4):
                        pe.wait_ge(S["n_ready"], b * TILES + 4 * (hf + 1))
                        src, c = (n, a)[w // 2], w % 2
                        for t in range(4):
                            last = nc.tensor.transpose(ps[:, 4 * hf + w, t * P:(t + 1) * P],
                                                       src[:, 4 * hf + t, c * P:(c + 1) * P], ident[:])
                        last.then_inc(S["tr_mm"], 1)

                def qk_jobs(g):
                    for hf in range(2):
                        for w in range(2):
                            job = 4 * g + 2 * hf + w
                            if g == 0:
                                pe.wait_ge(S["nt_ready"], b * 4 + 2 * (hf + 1))
                                if job >= 2:
                                    pe.wait_ge(S["at_ready"], b * 4 + 2)
                            else:
                                pe.wait_ge(S["v_ready"], b * 4 + 2 * hf + w + 1)
                            for c in range(DC):
                                last = mm(ps[:, job, :], wqk[:, c, w * D + g * P:w * D + (g + 1) * P],
                                          nt[:, c, hf * HALF:(hf + 1) * HALF], start=(c == 0), stop=(c == DC - 1))
                            last.then_inc(S["qk_mm"], 1)

                qk_jobs(0)
                for j in range(4):
                    pe.wait_ge(S["at_ready"], b * 4 + 4)
                    for t in range(2):
                        for c in range(DC):
                            last = mm(ps[:, 4 + j, t * D:(t + 1) * D], nt[:, c, (2 * j + t) * P:(2 * j + t + 1) * P],
                                      wv[:, c, :], start=(c == 0), stop=(c == DC - 1), skip_group_check=True)
                    last.then_inc(S["v_mm"], 1)
                for c2 in range(DC):
                    for hf in range(2):
                        pe.wait_ge(S["qk_lo"], b * 8 + 2 * c2 + hf + 1)
                        for c in range(DC):
                            last = mm(ps[:, 2 * c2 + hf, :], wg[:, c, c2 * P:(c2 + 1) * P],
                                      at[:, c, hf * HALF:(hf + 1) * HALF], start=(c == 0), stop=(c == DC - 1))
                        last.then_inc(S["g_mm"], 1)
                qk_jobs(1)

                def score(k):
                    g, i, hh = k // 32, (k % 32) // 4, k % 4
                    if k == 0:
                        pe.wait_ge(S["stack0"], (b * 24 + 24) * 16)
                        pe.wait_ge(S["g_exp"], b * 4 + 4)
                    if k == 2:
                        pe.wait_ge(S["qk_lo"], b * 8 + 8)
                    if k == 32:
                        pe.wait_ge(S["stack1"], (b * 24 + 24) * 16)
                    if k >= SR:
                        pe.wait_ge(S["exp_done"], b * STEPS + k - SR + 1)
                    for j in range(2):
                        last = mm(ps[:, 2 * (k % SR) + j, :], stq[:, 4 * g + hh, i * P:(i + 1) * P],
                                  stk[:, 4 * g + hh, j * 512:(j + 1) * 512], start=True, stop=True)
                    last.then_inc(S["score_mm"], 1)

                def weigh(gi):
                    g, i = gi // TILES, gi % TILES
                    pe.wait_ge(S["vs_ready"], b * 16 + gi + 1)
                    if gi == TILES:
                        pe.wait_ge(S["og_ready"], b * 4 + 2)
                    for j in range(2):
                        for hh in range(4):
                            k = 4 * gi + hh
                            last = mm(ps[32 * hh:32 * hh + 32, 6 + j, :], vs[:, gi % 2, hh, :],
                                      pr[:, k % PR, j * 512:(j + 1) * 512], start=(i == 0), stop=(i == TILES - 1))
                    last.then_inc(S["pv_mm"], 1)

                for k in range(STEPS):
                    score(k)
                    if k >= 6 and k % 4 == 2:
                        weigh((k - 6) // 4)
                weigh(15)

                pe.wait_ge(S["og_ready"], b * 4 + 4)
                for j in range(4):
                    for t in range(2):
                        for c in range(DC):
                            last = mm(ps[:, j, t * D:(t + 1) * D], og[:, c, (2 * j + t) * P:(2 * j + t + 1) * P],
                                      wfin[:, c, :], start=(c == 0), stop=(c == DC - 1), skip_group_check=True)
                    last.then_inc(S["fin_mm"], 1)
                for hf in range(2):
                    for c in range(DC):
                        pe.wait_ge(S["xn_ready"], b * TILES + 4 * (hf + 1))
                        for t in range(4):
                            last = nc.tensor.transpose(ps[:, 4 + 2 * hf + c, t * P:(t + 1) * P],
                                                       n[:, 4 * hf + t, c * P:(c + 1) * P], ident[:])
                        last.then_inc(S["xt_mm"], 1)
                for hf in range(2):
                    pe.wait_ge(S["xt_ready"], b * 4 + 2 * (hf + 1))
                    for k in range(HC):
                        if hf == 0 and k >= 6:
                            pe.wait_ge(S["xt_ready"], b * 4 + 4)
                        if hf == 1:
                            pe.wait_ge(S["ff_act"], b * 16 + k + 1)
                        for c in range(DC):
                            last = mm(ps[:, k, :], wf1[:, c, k * P:(k + 1) * P],
                                      nt[:, c, hf * HALF:(hf + 1) * HALF], start=(c == 0), stop=(c == DC - 1))
                        last.then_inc(S["ff_mm"], 1)
                for hf in range(2):
                    pe.wait_ge(S["ff_act"], b * 16 + 16)
                    for k in range(HC):
                        cg = 32 * (k % 4)
                        last = mm(ps[cg:cg + 32, 6 * hf + hf, :] if hf else ps[cg:cg + 32, 6, :], wr[:, k, :], ht[hf][:, k, :],
                                  start=(k < 4), stop=(k >= 4))
                    last.then_inc(S["lg_mm"], 1)
                for hf in range(2):
                    pe.wait_ge(S["lt_ready"], b * 2 + hf + 1)
                    for t in range(4):
                        last = mm(ps[:, hf, t * EXPERTS:(t + 1) * EXPERTS], lt[:, t * P:(t + 1) * P], pick[:],
                                  start=True, stop=True)
                    last.then_inc(S["lg2_mm"], 1)

            pe.wait_ge(S["r_oh"], 1)
            pe.wait_ge(S["c_consts"], 16 * 6)
            oh_flat = oh[:].rearrange("p t e -> p (t e)")
            mm(ps[:, 0, :], up[:], oh_flat, start=True, stop=True)
            mm(ps[:, 1, :], ones[:], oh_flat, start=True, stop=True).then_inc(S["r_mm"], 1)
            pe.wait_ge(S["slots_ready"], 1)
            pe.wait_ge(S["wd_in"], 16 * EXPERTS)
            with pe.Fori(0, SORT_GROUPS // 2) as g2:
                for i in range(2):
                    pe.wait_ge([S["xg_in0"], S["xg_in1"]][i], (g2 + 1) * 16 * GROUP)
                    pe.wait_ge(S["gf_act"], g2 * 16 + 8 * i)
                    for c in range(DC):
                        for t in range(GROUP):
                            last = nc.tensor.transpose(ps[:, c, t * P:(t + 1) * P],
                                                       xg[:, i, t, c * P:(c + 1) * P], ident[:])
                        last.then_inc(S["gt_mm"], 1)
                    pe.wait_ge(S["gt_ready"], g2 * 4 + 2 * i + 2)
                    for k in range(HC):
                        if k >= 4:
                            pe.wait_ge(S["gf_act"], g2 * 16 + 8 * i + k - 3)
                        for c in range(DC):
                            last = mm(ps[:, 2 + k % 4, :], wf1[:, c, k * P:(k + 1) * P], xgt[:, i, c, :],
                                      start=(c == 0), stop=(c == DC - 1))
                        last.then_inc(S["gf_mm"], 1)
                    pe.wait_ge(S["gf_act"], g2 * 16 + 8 * i + 8)
                    pe.wait_ge(S["y_ready"], g2 * 4 + 2 * i)
                    for t in range(GROUP):
                        e = pe.value_load(slot_expert[0:1, bass.ds(g2 * (2 * GROUP) + i * GROUP + t, 1)],
                                          min_val=0, max_val=EXPERTS - 1)
                        o = ps[:, 6 + t // 2, (t % 2) * D:(t % 2 + 1) * D]
                        for k in range(HC):
                            mm(o, hg[:, i, k, t * P:(t + 1) * P], wd[:, bass.ds(e, 1), k, :],
                               start=(k == 0), stop=False, skip_group_check=True)
                        last = mm(o, ones[0:1, :], bd[0:1, bass.ds(e, 1), :], start=False, stop=True, skip_group_check=True)
                        if t % 2:
                            last.then_inc(S["y_mm"], 1)

        @block.scalar
        def _(act):
            actv = nc.scalar.activation
            for j in range(4):
                act.wait_ge(S["pos_mm"], j + 1)
                actv(posr[:, j // 2, (j % 2) * HALF:(j % 2 + 1) * HALF], ps[:, j, :], ACT.Relu).then_inc(S["pos_relu"], 1)
            for j in range(4):
                act.wait_ge(S["pos_mm2"], 2 * j + 2)
                actv(posb[:, 2 * j:2 * j + 2, :].rearrange("p t d -> p (t d)"), ps[:, 4 + j, :], ACT.Identity
                     ).then_inc(S["pos_done"], 1)
            with act.Fori(0, IMAGES) as b:
                for hf in range(2):
                    for c in range(DC):
                        act.wait_ge(S["tr_mm"], b * 8 + 4 * hf + c + 1)
                        actv(nt[:, c, hf * HALF:(hf + 1) * HALF], ps[:, 4 * hf + c, :], ACT.Identity,
                             bias=beta[:, c:c + 1], scale=gamma[:, c:c + 1]).then_inc(S["nt_ready"], 1)

                def qk_hi(g):
                    for hf in range(2):
                        for w in range(2):
                            job = 4 * g + 2 * hf + w
                            act.wait_ge(S["qk_mm"], b * 8 + job + 1)
                            if job == 4:
                                act.wait_ge(S["stack0"], (b * 24 + 24) * 16)
                            actv(qk[:, w, 0, hf * HALF:(hf + 1) * HALF], ps[:, job, :], ACT.Identity,
                                 scale=(SCALE if w == 0 else 1.0)).then_inc(S["qk_hi"], 1)

                qk_hi(0)
                for j in range(4):
                    act.wait_ge(S["v_mm"], b * 4 + j + 1)
                    actv(v[:, 2 * j:2 * j + 2, :].rearrange("p t d -> p (t d)"), ps[:, 4 + j, :], ACT.Identity
                         ).then_inc(S["v_ready"], 1)
                for c in range(DC):
                    for hf in range(2):
                        act.wait_ge(S["g_mm"], b * 4 + 2 * c + hf + 1)
                        if c == 0 and hf == 0:
                            act.wait_ge(S["ha_ready"], b + 1)
                        actv(gate[:, c, hf * HALF:(hf + 1) * HALF], ps[:, 2 * c + hf, :], ACT.Exp,
                             bias=nbgate[:, c:c + 1], scale=-1.0).then_inc(S["g_exp"], 1)
                qk_hi(1)
                for k in range(STEPS):
                    act.wait_ge(S["max_done"], b * STEPS + k + 1)
                    if k >= PR:
                        act.wait_ge(S["pv_mm"], b * 16 + (k - PR) // 4 + 1)
                    actv(pr[:, k % PR, :], ps[:, 2 * (k % SR):2 * (k % SR) + 2, :].rearrange("p a n -> p (a n)"),
                         ACT.Exp, bias=nmax[:, k % 16:k % 16 + 1], accum_out=rsum[:, k % 16:k % 16 + 1]
                         ).then_inc(S["exp_done"], 1)
                for hf in range(2):
                    for k in range(HC):
                        act.wait_ge(S["ff_mm"], b * 16 + 8 * hf + k + 1)
                        actv(ht[hf][:, k, :], ps[:, k, :], ACT.Gelu, bias=bf1[:, k:k + 1]).then_inc(S["ff_act"], 1)
            act.wait_ge(S["r_exp"], 1)
            actv(ee[:], ee[:], ACT.Exp).then_inc(S["r_exp"], 1)
            with act.Fori(0, SORT_GROUPS // 2) as g2:
                for i in range(2):
                    for k in range(HC):
                        act.wait_ge(S["gf_mm"], g2 * 16 + 8 * i + k + 1)
                        if k == 0:
                            act.wait_ge(S["y_mm"], g2 * 4 + 2 * i)
                        actv(hg[:, i, k, :], ps[:, 2 + k % 4, :], ACT.Gelu, bias=bf1[:, k:k + 1]).then_inc(S["gf_act"], 1)

        @block.vector
        def _(dve):
            V = nc.vector
            chain = [0]

            def mark(ins):
                chain[0] += 1
                return ins.then_inc(S["vec_chain"], 1)

            def sync(base=0):
                hold(dve, S["vec_chain"], base + chain[0])

            V.memset(ones[:], 1.0).then_inc(S["setup"], 1)
            dve.wait_ge(S["consts"], 16 * 18)
            mark(V.tensor_scalar(nbgate[:], bgate, -1.0, None, ALU.mult))
            sync()
            before = chain[0]
            PER = 3 * (2 * TILES - 1) + 16

            with dve.Fori(0, IMAGES) as b:
                chain[0] = before
                base = b * PER

                def stats(src):
                    for t in range(TILES):
                        mark(V.bn_stats(bst[:, t, :], src[:, t, :]))
                    sync(base)
                    for t in range(TILES):
                        last = V.bn_aggr(mv[:, t, :], bst[:, t, :])
                        if t < TILES - 1:
                            mark(last)
                    last.then_inc(S["var_ready"], 1)

                def normalise(dst, src, done, ln):
                    dve.wait_ge(S["rstd_ready"], b * 3 + ln + 1)
                    for t in range(TILES):
                        V.tensor_scalar(dst[:, t, :], src[:, t, :], mv[:, t, 0:1], rstd[:, t:t + 1],
                                        ALU.subtract, ALU.mult).then_inc(done, 1)

                dve.wait_ge(S["h_out"], b * 16)
                for t in range(TILES):
                    dve.wait_ge(S["emb_mm"], b * TILES + t + 1)
                    V.tensor_tensor(h[:, t, :], ps[:, t, 0:D], posb[:, t, :], ALU.add).then_inc(S["emb_h"], 1)
                dve.wait_ge(S["emb_h"], b * TILES + TILES)
                stats(h)
                normalise(a, h, S["a_ready"], 0)
                dve.wait_ge(S["a_ready"], b * TILES + TILES)
                stats(a)
                dve.wait_ge(S["xn_out"], b * 16)
                normalise(n, a, S["n_ready"], 1)
                for hf in range(2):
                    for c in range(DC):
                        dve.wait_ge(S["tr_mm"], b * 8 + 4 * hf + 2 + c + 1)
                        V.tensor_copy(at[:, c, hf * HALF:(hf + 1) * HALF], ps[:, 4 * hf + 2 + c, :]).then_inc(S["at_ready"], 1)

                def qk_lo(g):
                    for hf in range(2):
                        for w in range(2):
                            job = 4 * g + 2 * hf + w
                            dve.wait_ge(S["qk_hi"], b * 8 + job + 1)
                            V.scalar_tensor_tensor(
                                qk[:, w, 1, hf * HALF:(hf + 1) * HALF], ps[:, job, :], SCALE if w == 0 else 1.0,
                                qk[:, w, 0, hf * HALF:(hf + 1) * HALF].bitcast(F32), ALU.mult, ALU.subtract
                            ).then_inc(S["qk_lo"], 1)

                qk_lo(0)
                qk_lo(1)
                for c in range(DC):
                    for hf in range(2):
                        piece = gate[:, c, hf * HALF:(hf + 1) * HALF]
                        dve.wait_ge(S["g_one"], b * 4 + 2 * c + hf + 1)
                        V.reciprocal(piece, piece).then_inc(S["g_ready"], 1)

                def scale_v(gi):
                    g, i = gi // TILES, gi % TILES
                    col = (4 * gi) % 16
                    dve.wait_ge(S["exp_done"], b * STEPS + 4 * gi + 4)
                    if gi >= 2:
                        dve.wait_ge(S["pv_mm"], b * 16 + gi - 1)
                    mark(V.reciprocal(rinv[:, gi % 2, :], rsum[:, col:col + 4]))
                    sync(base)
                    V.tensor_tensor(vs[:, gi % 2], v[:, i, g * P:(g + 1) * P].rearrange("p (a d) -> p a d", a=4),
                                    rinv[:, gi % 2, :, None].broadcast_to([P, 4, HD]), ALU.mult).then_inc(S["vs_ready"], 1)

                def gated(g):
                    for j in range(2):
                        dve.wait_ge(S["pv_mm"], b * 16 + 8 * (g + 1))
                        dve.wait_ge(S["g_ready"], b * 4 + 4)
                        V.tensor_tensor(og[:, g, j * 512:(j + 1) * 512], ps[:, 6 + j, :],
                                        gate[:, g, j * 512:(j + 1) * 512], ALU.mult).then_inc(S["og_ready"], 1)

                for k in range(STEPS):
                    dve.wait_ge(S["score_mm"], b * STEPS + k + 1)
                    V.reduce_max(nmax[:, k % 16:k % 16 + 1], ps[:, 2 * (k % SR):2 * (k % SR) + 2, :].rearrange("p a n -> p (a n)"),
                                 AX_X, negate=True).then_inc(S["max_done"], 1)
                    if k >= 5 and k % 4 == 1:
                        scale_v((k - 5) // 4)
                    if k == 36:
                        gated(0)
                scale_v(15)
                gated(1)
                for j in range(4):
                    dve.wait_ge(S["fin_mm"], b * 4 + j + 1)
                    dve.wait_ge(S["ha_ready"], b + 1)
                    V.tensor_tensor(h_flat[:, j * 512:(j + 1) * 512], h_flat[:, j * 512:(j + 1) * 512], ps[:, j, :], ALU.add
                                    ).then_inc(S["fin_h"], 1)
                dve.wait_ge(S["fin_h"], b * 4 + 4)
                stats(h)
                normalise(n, h, S["xn_ready"], 2)
                for j in range(4):
                    dve.wait_ge(S["xt_mm"], b * 4 + j + 1)
                    V.tensor_copy(nt[:, j % 2, (j // 2) * HALF:(j // 2 + 1) * HALF], ps[:, 4 + j, :]).then_inc(S["xt_ready"], 1)
                for hf in range(2):
                    dve.wait_ge(S["lg_mm"], b * 2 + hf + 1)
                    if hf == 1:
                        dve.wait_ge(S["lg2_mm"], b * 2 + 1)
                    V.tensor_copy(lt[:], ps[:, 6 + hf, :]).then_inc(S["lt_ready"], 1)
                    dve.wait_ge(S["lg2_mm"], b * 2 + hf + 1)
                    V.tensor_copy(logits[:, bass.ds(b * TILES + 4 * hf, 4), :],
                                  ps[:, hf, 0:4 * EXPERTS].rearrange("p (t e) -> p t e", e=EXPERTS)).then_inc(S["lg_done"], 1)
            assert chain[0] - before == 3 * (2 * TILES - 1) + 16, chain[0] - before

            b0 = IMAGES * (3 * (2 * TILES - 1) + 16)

            def link(ins):
                mark(ins)
                dve.wait_ge(S["vec_chain"], b0 - (chain_end - before) + chain[0])
            chain_end = chain[0]
            b0 += 0

            wide = [P, ALL_TILES, EXPERTS]
            dve.wait_ge(S["lg_done"], 2 * IMAGES)
            dve.wait_ge(S["c_consts"], 16 * 6)
            link(V.tensor_tensor(logits[:], logits[:], brt[:], ALU.add))
            link(V.reduce_max(red[:, 0, :], logits[:], AX_X))
            V.tensor_tensor(ee[:], logits[:], red[:, 0, :, None].broadcast_to(wide), ALU.subtract).then_inc(S["r_exp"], 1)
            dve.wait_ge(S["r_exp"], 2)
            link(V.reduce_max(red[:, 1, :], ee[:], AX_X))
            link(V.reduce_sum(red[:, 2, :], ee[:], AX_X))
            link(V.reciprocal(red[:, 2, :], red[:, 2, :]))
            link(V.tensor_tensor(prob[:], red[:, 1, :], red[:, 2, :], ALU.mult))
            link(V.tensor_tensor(oh[:], ee[:], red[:, 1, :, None].broadcast_to(wide), ALU.is_ge))
            link(V.tensor_tensor(oh[:], oh[:], rnk[:], ALU.mult))
            link(V.reduce_max(red[:, 3, :], oh[:], AX_X))
            V.tensor_tensor(oh[:], oh[:], red[:, 3, :, None].broadcast_to(wide), ALU.is_equal).then_inc(S["r_oh"], 1)
            link(V.memset(onesf[:], 1.0))
            dve.wait_ge(S["r_mm"], 1)
            link(V.tensor_copy(tot[:].rearrange("p t e -> p (t e)"), ps[:, 1, :]))
            for e in range(EXPERTS):
                mark(V.tensor_tensor_scan(run[:, :, e], onesf[:], tot[:, :, e], 0.0, ALU.mult, ALU.add))
            link(V.memset(slot_f[:], 0.0))
            link(V.tensor_scalar(cnt_i[:, 0, :], run[:, ALL_TILES - 1, :], float(P - 1), None, ALU.add))
            link(V.tensor_scalar(cnt_i[:, 1, :], cnt_i[:, 0, :], 7, 7, ALU.arith_shift_right, ALU.logical_shift_left))
            link(V.tensor_copy(cnt[:, 0, :], cnt_i[:, 1, :]))
            link(V.tensor_tensor_scan(cnt[:, 1, :], onesf[:, 0:EXPERTS], cnt[:, 0, :], 0.0, ALU.mult, ALU.add))
            link(V.tensor_tensor(cnt[:, 2, :], cnt[:, 1, :], cnt[:, 0, :], ALU.subtract))
            link(V.tensor_tensor(run[:], run[:], tot[:], ALU.subtract))
            link(V.tensor_tensor(run[:].rearrange("p t e -> p (t e)"), run[:].rearrange("p t e -> p (t e)"), ps[:, 0, :], ALU.add))
            link(V.tensor_tensor(run[:], run[:], cnt[:, 2, None, :].broadcast_to(wide), ALU.add))
            link(V.tensor_tensor(run[:], run[:], oh[:], ALU.mult))
            link(V.reduce_sum(place_f[:], run[:], AX_X))
            link(V.tensor_copy(place_i[:], place_f[:]))
            link(V.tensor_scalar(place_a[:, 0, :], place_i[:], P - 1, None, ALU.bitwise_and))
            link(V.tensor_scalar(place_a[:, 1, :], place_i[:], 7, None, ALU.arith_shift_right))
            link(V.scalar_tensor_tensor(place_a[:, 2, :], place_a[:, 0, :], float(SLOTS), place_a[:, 1, :], ALU.mult, ALU.add))
            for e in range(EXPERTS):
                link(V.scalar_tensor_tensor(slot_f[:, (e + 1) % 2, :], sst[:], cnt[:, 1, e:e + 1], slot_f[:, e % 2, :],
                                            ALU.is_ge, ALU.add))
            V.tensor_scalar(slot_expert[:], slot_f[:, EXPERTS % 2, :], float(EXPERTS - 1), None, ALU.min).then_inc(S["slots_ready"], 1)
            with dve.Fori(0, ALL_TILES // 16) as j2:
                for i in range(2):
                    dve.wait_ge([S["inv_out0"], S["inv_out1"]][i], j2 * 128)
                    mark(V.tensor_copy(inv_tok[:, i], tid[:, bass.ds(j2 * 16 + 8 * i, 8)]))
                    dve.wait_ge(S["vec_chain"], b0 - (chain_end - before) + chain[0] + j2 * 2)
                    V.tensor_copy(inv_pos[:, i], place_a[:, 2, bass.ds(j2 * 16 + 8 * i, 8)]).then_inc(S["inv_stage"], 1)
            with dve.Fori(0, SORT_GROUPS // 2) as g2:
                for i in range(2):
                    for c in range(DC):
                        dve.wait_ge(S["gt_mm"], g2 * 4 + 2 * i + c + 1)
                        V.tensor_copy(xgt[:, i, c, :], ps[:, c, :]).then_inc(S["gt_ready"], 1)
                    dve.wait_ge([S["y_out0"], S["y_out1"]][i], g2 * 16)
                    for j in range(2):
                        dve.wait_ge(S["y_mm"], g2 * 4 + 2 * i + j + 1)
                        V.tensor_copy(yo[:, i, 2 * j:2 * j + 2, :].rearrange("p t d -> p (t d)"), ps[:, 6 + j, :]
                                      ).then_inc(S["y_ready"], 1)
            with dve.Fori(0, IMAGES // 2) as j2:
                for i in range(2):
                    V.tensor_copy(pcol[:, i], prob[:, bass.ds(j2 * 16 + 8 * i, 8)]).then_inc(S["pcol_ready"], 1)
                    dve.wait_ge(S["pcol_ready"], j2 * 2 + i + 1)
                    dve.wait_ge([S["yg_in0"], S["yg_in1"]][i], (j2 + 1) * 128)
                    dve.wait_ge([S["hr_in0"], S["hr_in1"]][i], (j2 + 1) * 16)
                    for k in range(8):
                        last = V.scalar_tensor_tensor(yg[:, i, k, :], yg[:, i, k, :], pcol[:, i, k:k + 1], hr[:, i, k, :],
                                                      ALU.mult, ALU.add)
                    last.then_inc(S["o_ready"], 1)


def kernel(**inputs):
    import numpy as np
    import concourse.bacc as bacc
    from concourse.bass_utils import run_bass_kernel_spmd

    c = np.ascontiguousarray

    def chunked(w):
        return c(w.reshape(-1, P, w.shape[-1]).transpose(1, 0, 2))

    a = {k: np.asarray(v) for k, v in inputs.items()}
    x = a["x"].reshape(IMAGES, 3, 32, 16, 32, 16).transpose(0, 1, 3, 5, 2, 4).reshape(IMAGES, KC, P, 4, QUARTER)
    x = x.transpose(0, 3, 2, 1, 4)
    x = c(np.concatenate([x, np.zeros_like(x[:1])], 0))
    f32 = np.float32
    grid = np.arange(32, dtype=f32) / f32(31)
    pos_in = np.stack([np.repeat(grid, 32), np.tile(grid, 32), np.ones(TOKENS, f32)])
    w_qkv = a["L0_attn_W_qkv"].T
    router = np.concatenate([a["L0_ffn_Wg"], np.zeros((HID, 32 - EXPERTS), f32)], 1)
    pick = np.tile(np.concatenate([np.eye(EXPERTS, dtype=f32), np.zeros((32 - EXPERTS, EXPERTS), f32)]), (4, 1))
    rank = np.tile((EXPERTS - np.arange(EXPERTS, dtype=f32)), (P, ALL_TILES, 1))
    rank = np.concatenate([rank, np.repeat(pick[:, None, :], ALL_TILES, 1)], 2)
    tid = (np.arange(ALL_TILES)[None, :] * P + np.arange(P)[:, None]).astype(np.int32)
    tid = np.concatenate([tid, np.zeros((P, SLOTS), np.int32)], 1)
    arrays = {
        "x_in": x,
        "w_patch": chunked(a["L0_tok_Wp"]),
        "pos_in": c(pos_in),
        "pos_w1": c(np.concatenate([a["L0_tok_W1"], a["L0_tok_b1"][None]], 0)),
        "pos_w2": chunked(a["L0_tok_W2"]),
        "pos_bias": c(np.stack([a["L0_tok_b2"], a["L0_tok_bp"]])),
        "ln_gamma": c(a["L0_attn_ln_gamma"].reshape(DC, P).T),
        "ln_beta": c(a["L0_attn_ln_beta"].reshape(DC, P).T),
        "w_qk": chunked(w_qkv[:, :2 * D]),
        "w_v": chunked(w_qkv[:, 2 * D:]),
        "w_gate": chunked(a["L0_attn_W_gate"].T),
        "b_gate": c(a["L0_attn_b_gate"].reshape(DC, P).T),
        "w_final": chunked(a["L0_attn_W_final"].T),
        "b_final": c(np.tile(a["L0_attn_b_final"], (P, 1))),
        "w_ffn1": chunked(a["L0_ffn_W1"]),
        "b_ffn1": c(a["L0_ffn_b1"].reshape(HC, P).T),
        "w_router": chunked(router),
        "b_router": c(np.tile(a["L0_ffn_bg"], (P, ALL_TILES, 1))),
        "w_down": c(a["L0_ffn_Wd"].reshape(EXPERTS, HC, P, D).transpose(0, 2, 1, 3)),
        "b_down": c(a["L0_ffn_bd"][None]),
        "identity": np.eye(P, dtype=f32),
        "upper": np.triu(np.ones((P, P), f32), 1),
        "rank": c(rank),
        "slot_start": c(np.tile(np.arange(SLOTS, dtype=f32) * P, (P, 1))),
        "token_id": c(tid),
    }
    nc = bacc.Bacc("TRN2", target_bir_lowering=False, num_devices=1)
    aps = [nc.dram_tensor(k, v.shape, mybir.dt.from_np(v.dtype), kind="ExternalInput").ap() for k, v in arrays.items()]
    aps.append(nc.dram_tensor("out", (IMAGES, TOKENS, D), F32, kind="ExternalOutput").ap())
    vit_layer_kernel(nc, *aps)
    r = run_bass_kernel_spmd(nc, [arrays], core_ids=[0])
    return r.results[0]["out"]
```

```python
from contextlib import ExitStack

import concourse.bass as bass
from concourse import mybir

F32 = mybir.dt.float32
F32R = mybir.dt.float32r
I32 = mybir.dt.int32
ALU = mybir.AluOpType
ACT = mybir.ActivationFunctionType
AX_X = mybir.AxisListType.X

P = 128
IMAGES = 8
TOKENS = 1024
TILES = TOKENS // P
ALL_TILES = IMAGES * TILES
D = 256
DC = D // P
KC = 3 * 16 * 16 // P
HALF = TOKENS // 2
HEADS, HD = 8, 32
GROUPS = HEADS // 4
STEPS = HEADS * TILES
HID = 1024
HC = HID // P
EXPERTS = 8
SLOTS = ALL_TILES + EXPERTS
GROUP = 4
SORT_GROUPS = SLOTS // GROUP
G_STEPS = STEPS // GROUPS
PR = 8
SR = 2
O_BANK, SPARE = 4, 6
EPS = 1e-5
SCALE = float(HD) ** -0.5


def vit_layer_kernel(nc, x, w_patch, pos_in, pos_w1, pos_w2, pos_bias, ln_gamma, ln_beta, w_qk, w_v,
                     w_gate, b_gate, w_final, b_final, w_ffn1, b_ffn1, w_router, b_router, w_down,
                     b_down, identity, upper, rank, slot_start, token_id, out):
    xn_rows = nc.dram_tensor("xn_rows", (ALL_TILES * P, D), F32).ap()
    h_rows = nc.dram_tensor("h_rows", (ALL_TILES * P, D), F32).ap()
    y_rows = nc.dram_tensor("y_rows", (SLOTS * P, D), F32).ap()
    sorted_ids = nc.dram_tensor("sorted_ids", (SLOTS * P, 1), I32).ap()

    h_view = h_rows.rearrange("(b t p) d -> b p t d", b=IMAGES, t=TILES)
    xn_view = xn_rows.rearrange("(b t p) d -> b p t d", b=IMAGES, t=TILES)
    y_view = y_rows.rearrange("(g t p) d -> g p t d", t=GROUP, p=P)
    out_view = out.rearrange("b (t p) d -> b p t d", p=P)

    with ExitStack() as ctx:
        def sem(name):
            return ctx.enter_context(nc.semaphore(name))

        def tensor(stack, name, shape, dt=F32):
            return stack.enter_context(nc.sbuf_tensor(name, shape, dt))

        ps = ctx.enter_context(nc.psum_tensor("ps", [P, 8, 512], F32))

        ident = tensor(ctx, "ident", [P, P])
        wf1 = tensor(ctx, "wf1", [P, DC, HID])
        bf1 = tensor(ctx, "bf1", [P, HC])
        ones = tensor(ctx, "ones", [P, P])
        logits = tensor(ctx, "logits", [P, ALL_TILES, EXPERTS])

        sa = ExitStack()
        wp = tensor(sa, "wp", [P, KC, D])
        wqk = tensor(sa, "wqk", [P, DC, 2 * D])
        wv = tensor(sa, "wv", [P, DC, D])
        wg = tensor(sa, "wg", [P, DC, D])
        wfin = tensor(sa, "wfin", [P, DC, D])
        wr = tensor(sa, "wr", [P, HC, 32])
        posb = tensor(sa, "posb", [P, TILES, D])
        vecs = tensor(sa, "vecs", [P, 3, DC])
        gamma, beta, bgate = vecs[:, 0, :], vecs[:, 1, :], vecs[:, 2, :]
        nbgate = tensor(sa, "nbgate", [P, DC])
        bfin = tensor(sa, "bfin", [P, D])
        pick = tensor(sa, "pick", [P, EXPERTS])
        xt = tensor(sa, "xt", [P, 2, KC, P])
        hres = tensor(sa, "hres", [P, 2, TILES, D])
        a = tensor(sa, "a", [P, TILES, D])
        n = tensor(sa, "n", [P, TILES, D])
        nt = tensor(sa, "nt", [P, DC, TOKENS])
        at = tensor(sa, "at", [P, DC, TOKENS])
        qk = tensor(sa, "qk", [P, 2, 2, TOKENS], F32R)
        stq = tensor(sa, "stq", [96, 4, TOKENS], F32R)
        stk = tensor(sa, "stk", [96, 4, TOKENS], F32R)
        v = tensor(sa, "v", [P, TILES, D])
        vs = tensor(sa, "vs", [P, 2, 4, HD])
        pr = tensor(sa, "pr", [P, PR, TOKENS])
        lt = tensor(sa, "lt", [P, HALF])
        bst = tensor(sa, "bst", [P, 3, TILES, 6])
        mv = tensor(sa, "mv", [P, 3, TILES, 2])
        rstd = tensor(sa, "rstd", [P, 3, TILES])
        vare = tensor(sa, "vare", [P, 3, TILES])
        half_neg = tensor(sa, "half_neg", [P, TILES])
        nmax = tensor(sa, "nmax", [P, 16])
        rsum = tensor(sa, "rsum", [P, 16])
        rinv = tensor(sa, "rinv", [P, 2, 4])
        gate = tensor(sa, "gate", [P, DC, TOKENS])
        ht = tensor(sa, "ht", [P, HC, HALF])
        posin = pr[0:3, 0, :]
        posw1 = pr[0:3, 1, 0:D]
        sa.close()

        sc = ExitStack()
        prob = tensor(sc, "prob", [P, ALL_TILES])
        place_i = tensor(sc, "place_i", [P, ALL_TILES], I32)
        slot_expert = tensor(sc, "slot_expert", [P, SLOTS], I32)
        wd = tensor(sc, "wd", [P, EXPERTS, HC, D])
        bd = tensor(sc, "bd", [1, EXPERTS, D])
        up = tensor(sc, "up", [P, P])
        rnk = tensor(sc, "rnk", [P, ALL_TILES, EXPERTS])
        brt = tensor(sc, "brt", [P, ALL_TILES, EXPERTS])
        sst = tensor(sc, "sst", [P, SLOTS])
        tid = tensor(sc, "tid", [P, ALL_TILES], I32)
        ee = tensor(sc, "ee", [P, ALL_TILES, EXPERTS])
        oh = tensor(sc, "oh", [P, ALL_TILES, EXPERTS])
        tot = tensor(sc, "tot", [P, ALL_TILES, EXPERTS])
        run = tensor(sc, "run", [P, ALL_TILES, EXPERTS])
        red = tensor(sc, "red", [P, 4, ALL_TILES])
        onesf = tensor(sc, "onesf", [P, ALL_TILES])
        cnt_i = tensor(sc, "cnt_i", [P, 2, EXPERTS], I32)
        cnt = tensor(sc, "cnt", [P, 3, EXPERTS])
        slot_f = tensor(sc, "slot_f", [P, 2, SLOTS])
        place_f = tensor(sc, "place_f", [P, ALL_TILES])
        place_a = tensor(sc, "place_a", [P, 3, ALL_TILES], I32)
        inv_pos = tensor(sc, "inv_pos", [P, 2, 8], I32)
        inv_tok = tensor(sc, "inv_tok", [P, 2, 8], I32)
        inv = tensor(sc, "inv", [P, SLOTS], I32)
        idx = tensor(sc, "idx", [P, 2, GROUP], I32)
        xg = tensor(sc, "xg", [P, 2, GROUP, D])
        xgt = tensor(sc, "xgt", [P, 2, DC, 512])
        hg = tensor(sc, "hg", [P, 2, HC, 512])
        yo = tensor(sc, "yo", [P, 2, GROUP, D])
        back = tensor(sc, "back", [P, 2, 8], I32)
        pcol = tensor(sc, "pcol", [P, 2, 8])
        yg = tensor(sc, "yg", [P, 2, 8, D])
        hr = tensor(sc, "hr", [P, 2, 8, D])
        sc.close()

        S = {}
        for name in ("consts setup pos_mm pos_relu pos_mm2 pos_done x_in0 x_in1 emb_mm emb_h "
                     "stats1 stats2 stats3 var1 var2 var3 eps1 eps2 eps3 rstd1 rstd2 rstd3 pow_ready "
                     "a_ready n_ready xn_ready tr_mm tr_read h_sum ha_ready qk_mm qk_hi qk_lo v_mm v_read "
                     "g_mm g_exp g_one g_ready stack0 stack1 score_mm max_done exp_done rinv_done vs_ready "
                     "pv_mm og_ready fin_mm fin_h h_out xn_out xt_mm xt_read ff_mm ff_act lg_mm lt_ready "
                     "lg2_mm lg_done ids_zero c_consts wd_in chain r_exp r_oh r_mm slots_ready staged_tok "
                     "inv_stage inv_out0 inv_out1 inv_in idx_ready xg_in0 xg_in1 gt_mm gt_read gf_mm gf_act "
                     "y_mm y_ready y_out0 y_out1 back_idx yg_in0 yg_in1 hr_in0 hr_in1 pcol_ready o_ready "
                     "o_out0 o_out1").split():
            S[name] = sem(name)

        def both(name):
            return S[name + "0"], S[name + "1"]

        x_in, stacked = both("x_in"), both("stack")
        xg_in, y_out, yg_in, hr_in, o_out, inv_out = (both(k) for k in
                                                      ("xg_in", "y_out", "yg_in", "hr_in", "o_out", "inv_out"))
        posr = nt
        posw2 = at[:, 0, 0:DC * D].rearrange("p (c d) -> p c d", c=DC)
        posbias = at[0:2, 1, 0:D]
        N_CONSTS = 18

        def wait(eng, name, value):
            if not isinstance(value, int) or value > 0:
                eng.wait_ge(S[name] if isinstance(name, str) else name, value)

        def hold(eng, name, value):
            if not isinstance(value, int):
                value = eng.to_reg(value)
                eng.wait_ge(S["setup"], 1)
            wait(eng, name, value)

        def over_images(eng, body):
            body(0, 0, False, True)
            with eng.Fori(0, (IMAGES - 2) // 2) as j:
                body(j * 2 + 1, 1, True, True)
                body(j * 2 + 2, 0, True, True)
            body(IMAGES - 1, (IMAGES - 1) % 2, True, False)

        def over_groups(eng, body):
            body(0, 0)
            body(1, 1)
            with eng.Fori(1, SORT_GROUPS // 2) as j:
                body(j * 2, 0)
                body(j * 2 + 1, 1)

        def over_pairs(eng, count, body):
            body(0)
            with eng.Fori(1, count) as j:
                body(j)

        QK1_AT = {m: divmod(m, 2) for m in range(8)}
        EMBED_AT = {8 + m: divmod(m, 3) for m in range(24)}
        GATE_AT = {G_STEPS + 2 + m: divmod(m, 2) for m in range(4)}
        TURN_AT = {G_STEPS + 6 + j: j for j in range(8)}
        QK0_AT = {G_STEPS + 15 + 3 * j + c: (j, c) for j in range(4) for c in range(2)}
        LOW1_AT = {k + 2: j for k, (j, c) in QK1_AT.items() if c == 1}
        LOW0_AT = {k + 2: j for k, (j, c) in QK0_AT.items() if c == 1}
        NORM_AT = {2 + t: t for t in range(TILES)}
        INVERT_AT = {G_STEPS + 12 + 2 * q: q for q in range(8)}
        SCALE_AT = {4 * i + 5: i for i in range(15) if i != 7}
        WEIGH_AT = {4 * i + 6 + j: (i, j) for i in range(15) if i != 7 for j in range(2)}
        assert max(EMBED_AT) < G_STEPS and max(LOW0_AT) < STEPS

        block = ctx.enter_context(nc.Block())

        @block.sync
        def _(sp):
            for dst, src in ((posin, pos_in), (posw1, pos_w1), (posw2, pos_w2), (posbias, pos_bias),
                             (wp[:], w_patch), (ident[:], identity), (vecs[:, 0, :], ln_gamma),
                             (vecs[:, 1, :], ln_beta), (vecs[:, 2, :], b_gate), (wqk[:], w_qk), (wv[:], w_v),
                             (wg[:], w_gate), (wfin[:], w_final), (bfin[:], b_final), (wf1[:], w_ffn1),
                             (bf1[:], b_ffn1), (wr[:], w_router), (pick[:], rank[:, 0, EXPERTS:])):
                sp.dma_start(dst, src).then_inc(S["consts"], 16)
            sp.dma_start(sorted_ids.rearrange("(p q) o -> p (q o)", p=P), token_id[:, ALL_TILES:]
                         ).then_inc(S["ids_zero"], 16)

            def load_tile(b, t):
                sp.dma_start(xt[:, t % 2], x[b, t]).then_inc(x_in[t % 2], 16)

            def load_rest(b):
                for t in range(2, TILES):
                    hold(sp, "emb_mm", b * TILES + t - 1)
                    load_tile(b, t)

            def load_stack(b, g):
                hold(sp, "qk_lo", b * 8 + 4 * (g + 1))
                hold(sp, "score_mm", b * STEPS + g * G_STEPS)
                for hh in range(4):
                    for r in range(3):
                        src = slice(32 * hh, 32 * hh + 32)
                        dst = slice(32 * r, 32 * r + 32)
                        sp.dma_start(stq[dst, hh, :].bitcast(F32), qk[src, 0, r % 2, :].bitcast(F32)
                                     ).then_inc(stacked[g], 16)
                        sp.dma_start(stk[dst, hh, :].bitcast(F32), qk[src, 1, r // 2, :].bitcast(F32)
                                     ).then_inc(stacked[g], 16)

            load_tile(0, 0)
            load_tile(0, 1)
            load_rest(0)

            def image(b, par, before, after):
                load_stack(b, 0)
                if after:
                    for t in range(2):
                        hold(sp, "emb_mm", b * TILES + 7 + t)
                        load_tile(b + 1, t)
                    load_rest(b + 1)
                load_stack(b, 1)

            over_images(sp, image)
            sp.wait_ge(S["lg_done"], 2 * IMAGES)
            sp.wait_ge(S["h_out"], 16 * IMAGES)
            sp.wait_ge(S["xn_out"], 16 * IMAGES)
            for dst, src in ((up[:], upper), (rnk[:], rank[:, :, 0:EXPERTS]), (brt[:], b_router),
                             (sst[:], slot_start), (tid[:], token_id[:, 0:ALL_TILES]), (bd[:], b_down)):
                sp.dma_start(dst, src).then_inc(S["c_consts"], 16)
            for e in range(EXPERTS):
                sp.dma_start(wd[:, e], w_down[e]).then_inc(S["wd_in"], 16)
            for i in range(2):
                sp.wait_ge(inv_out[i], 16 * 8 * (ALL_TILES // 16))
            sp.dma_start(inv[:], sorted_ids.rearrange("(p q) o -> p (q o)", p=P)).then_inc(S["inv_in"], 16)

            def rows_out(g, i):
                hold(sp, "y_ready", g * 2 + 2)
                sp.dma_start(y_view[g], yo[:, i]).then_inc(y_out[i], 16)

            over_groups(sp, rows_out)

            def tokens_out(j):
                for i in range(2):
                    hold(sp, "o_ready", j * 2 + i - 1)
                    sp.dma_start(hr[:, i], h_view[j * 2 + i]).then_inc(hr_in[i], 16)
                for i in range(2):
                    hold(sp, "o_ready", j * 2 + i + 1)
                    sp.dma_start(out_view[j * 2 + i], yg[:, i]).then_inc(o_out[i], 16)

            over_pairs(sp, IMAGES // 2, tokens_out)
            for i in range(2):
                sp.wait_ge(o_out[i], 16 * (IMAGES // 2))
                sp.wait_ge(y_out[i], 16 * (SORT_GROUPS // 2))

        @block.gpsimd
        def _(pool):
            nc.gpsimd.memset(half_neg[:], -0.5).then_inc(S["pow_ready"], 1)
            pool.wait_ge(S["pow_ready"], 1)

            def root(ln, b):
                hold(pool, f"var{ln}", b + 1)
                nc.gpsimd.tensor_scalar(vare[:, ln - 1], mv[:, ln - 1, :, 1], EPS, None, ALU.add
                                        ).then_inc(S[f"eps{ln}"], 1)
                wait(pool, f"eps{ln}", b + 1)
                nc.gpsimd.tensor_tensor(rstd[:, ln - 1], vare[:, ln - 1], half_neg[:], ALU.pow
                                        ).then_inc(S[f"rstd{ln}"], 1)

            def front(b, par):
                root(1, b)
                root(2, b)
                h = hres[:, par]
                hold(pool, "n_ready", b + 1)
                nc.gpsimd.tensor_tensor(h, h, a[:], ALU.add).then_inc(S["h_sum"], 1)
                wait(pool, "h_sum", b + 1)
                nc.gpsimd.tensor_tensor(h, h, bfin[:, None, :].broadcast_to([P, TILES, D]), ALU.add
                                        ).then_inc(S["ha_ready"], 1)

            def add_one(b, c):
                for hf in range(2):
                    piece = gate[:, c, hf * HALF:(hf + 1) * HALF]
                    hold(pool, "g_exp", b * 4 + 2 * c + hf + 1)
                    nc.gpsimd.tensor_scalar(piece, piece, 1.0, None, ALU.add).then_inc(S["g_one"], 1)

            def store_rear(b, par):
                hold(pool, "fin_h", b * 4 + 4)
                nc.gpsimd.dma_start(h_view[b], hres[:, par]).then_inc(S["h_out"], 16)
                hold(pool, "xn_ready", b + 1)
                nc.gpsimd.dma_start(xn_view[b], n[:]).then_inc(S["xn_out"], 16)

            front(0, 0)

            def image(b, par, before, after):
                if before:
                    root(3, b - 1)
                add_one(b, 0)
                if before:
                    store_rear(b - 1, 1 - par)
                if after:
                    front(b + 1, 1 - par)
                add_one(b, 1)

            over_images(pool, image)
            root(3, IMAGES - 1)
            store_rear(IMAGES - 1, (IMAGES - 1) % 2)

            pool.wait_ge(S["ids_zero"], 16)

            def place_ids(j):
                for i in range(2):
                    hold(pool, "inv_stage", j * 2 + i + 1)
                    for k in range(8):
                        nc.gpsimd.indirect_dma_start(
                            sorted_ids, bass.IndirectOffsetOnAxis(inv_pos[:, i, k:k + 1], 0),
                            inv_tok[:, i, k:k + 1], None).then_inc(inv_out[i], 16)

            over_pairs(pool, ALL_TILES // 16, place_ids)
            pool.wait_ge(S["inv_in"], 16)

            def gather_rows(g, i):
                hold(pool, "gt_mm", g * 2 - 2)
                nc.gpsimd.tensor_copy(idx[:, i], inv[:, bass.ds(g * GROUP, GROUP)]).then_inc(S["idx_ready"], 1)
                hold(pool, "idx_ready", g + 1)
                for t in range(GROUP):
                    nc.gpsimd.indirect_dma_start(
                        xg[:, i, t, :], None, xn_rows,
                        bass.IndirectOffsetOnAxis(idx[:, i, t:t + 1], 0)).then_inc(xg_in[i], 16)

            over_groups(pool, gather_rows)

            for i in range(2):
                pool.wait_ge(y_out[i], 16 * (SORT_GROUPS // 2))

            def gather_tokens(j):
                for i in range(2):
                    hold(pool, o_out[i], j * 16)
                    nc.gpsimd.tensor_copy(back[:, i], place_i[:, bass.ds(j * 16 + 8 * i, 8)]
                                          ).then_inc(S["back_idx"], 1)
                    hold(pool, "back_idx", j * 2 + i + 1)
                    for k in range(8):
                        nc.gpsimd.indirect_dma_start(
                            yg[:, i, k, :], None, y_rows,
                            bass.IndirectOffsetOnAxis(back[:, i, k:k + 1], 0)).then_inc(yg_in[i], 16)

            over_pairs(pool, IMAGES // 2, gather_tokens)

        @block.tensor
        def _(pe):
            mm = nc.tensor.matmul

            def spare(j):
                return ps[:, SPARE + j % 2, :]

            pe.wait_ge(S["consts"], 16 * N_CONSTS)
            for c in range(DC):
                for hf in range(2):
                    mm(ps[:, 2 * c + hf, :], posw1[:, c * P:(c + 1) * P], posin[:, hf * HALF:(hf + 1) * HALF],
                       start=True, stop=True).then_inc(S["pos_mm"], 1)
            pe.wait_ge(S["pos_relu"], 4)
            pe.wait_ge(S["setup"], 1)
            for t in range(TILES):
                o = ps[:, 4 + t // 2, (t % 2) * D:(t % 2 + 1) * D]
                for c in range(DC):
                    mm(o, posr[:, c, t * P:(t + 1) * P], posw2[:, c, :], start=(c == 0), stop=False, skip_group_check=True)
                mm(o, ones[0:2, :], posbias, start=False, stop=True, skip_group_check=True).then_inc(S["pos_mm2"], 1)
            pe.wait_ge(S["pos_done"], 4)

            def embed(b, t, part):
                if part == 0:
                    wait(pe, x_in[t % 2], b * 64 + 16 * (t // 2 + 1))
                    if t >= 2:
                        wait(pe, "emb_h", b * TILES + t - 1)
                for k in range(2 * part, 2 * part + 2):
                    last = mm(spare(t)[:, 0:D], xt[:, t % 2, k, :], wp[:, k, :], start=(k == 0), stop=(k == KC - 1))
                if part == 2:
                    last.then_inc(S["emb_mm"], 1)

            def turn(b, j):
                hf, w = j // 4, j % 4
                wait(pe, "n_ready", b + 1)
                if j >= 2:
                    wait(pe, "tr_read", b * 8 + j - 1)
                src, c = (n, a)[w // 2], w % 2
                for t in range(4):
                    last = nc.tensor.transpose(spare(j)[:, t * P:(t + 1) * P],
                                               src[:, 4 * hf + t, c * P:(c + 1) * P], ident[:])
                last.then_inc(S["tr_mm"], 1)

            def project(b, g, j, c):
                hf, w = j // 2, j % 2
                if j >= 2 and c == 0:
                    wait(pe, "qk_lo", b * 8 + 4 * g + j - 1)
                last = mm(spare(j), wqk[:, c, w * D + g * P:w * D + (g + 1) * P],
                          nt[:, c, hf * HALF:(hf + 1) * HALF], start=(c == 0), stop=(c == DC - 1))
                if c == DC - 1:
                    last.then_inc(S["qk_mm"], 1)

            def score(b, k):
                g, i, hh = k // G_STEPS, (k % G_STEPS) // 4, k % 4
                if k % G_STEPS == 0:
                    wait(pe, stacked[g], (b * 24 + 24) * 16)
                if k >= SR:
                    wait(pe, "exp_done", b * STEPS + k - SR + 1)
                for j in range(2):
                    last = mm(ps[:, 2 * (k % SR) + j, :], stq[:, hh, i * P:(i + 1) * P],
                              stk[:, hh, j * 512:(j + 1) * 512], start=True, stop=True)
                last.then_inc(S["score_mm"], 1)

            def weigh(b, gi, j):
                i = gi % TILES
                if j == 0:
                    wait(pe, "vs_ready", b * 16 + gi + 1)
                    if i == 0:
                        wait(pe, "og_ready", b * 4 + 2 * (gi // TILES))
                for hh in range(4):
                    last = mm(ps[32 * hh:32 * hh + 32, O_BANK + j, :], vs[:, gi % 2, hh, :],
                              pr[:, (4 * gi + hh) % PR, j * 512:(j + 1) * 512],
                              start=(i == 0), stop=(i == TILES - 1))
                if j == 1:
                    last.then_inc(S["pv_mm"], 1)

            def values(b, pair):
                if pair == 0:
                    wait(pe, "qk_lo", b * 8 + 4)
                for j in (2 * pair, 2 * pair + 1):
                    if j >= 2:
                        wait(pe, "v_read", b * 4 + j - 1)
                    for t in range(2):
                        for c in range(DC):
                            last = mm(spare(j)[:, t * D:(t + 1) * D], nt[:, c, (2 * j + t) * P:(2 * j + t + 1) * P],
                                      wv[:, c, :], start=(c == 0), stop=(c == DC - 1), skip_group_check=True)
                    last.then_inc(S["v_mm"], 1)

            def gates(b, c2, hf, c):
                last = mm(spare(hf), wg[:, c, c2 * P:(c2 + 1) * P],
                          at[:, c, hf * HALF:(hf + 1) * HALF], start=(c == 0), stop=(c == DC - 1))
                if c == DC - 1:
                    last.then_inc(S["g_mm"], 1)

            def final(b):
                wait(pe, "og_ready", b * 4 + 4)
                for j in range(4):
                    if j >= 2:
                        wait(pe, "fin_h", b * 4 + j - 1)
                    elif isinstance(b, int) and b == IMAGES - 1:
                        wait(pe, "g_exp", b * 4 + 3 + j)
                    else:
                        wait(pe, "v_read", b * 4 + 7 + j)
                    for t in range(2):
                        for c in range(DC):
                            last = mm(spare(j)[:, t * D:(t + 1) * D], gate[:, c, (2 * j + t) * P:(2 * j + t + 1) * P],
                                      wfin[:, c, :], start=(c == 0), stop=(c == DC - 1), skip_group_check=True)
                    last.then_inc(S["fin_mm"], 1)

            def norm_turn(b):
                wait(pe, "xn_ready", b + 1)
                for j in range(4):
                    hf, c = j // 2, j % 2
                    if j >= 2:
                        wait(pe, "xt_read", b * 4 + j - 1)
                    for t in range(4):
                        last = nc.tensor.transpose(spare(j)[:, t * P:(t + 1) * P],
                                                   n[:, 4 * hf + t, c * P:(c + 1) * P], ident[:])
                    last.then_inc(S["xt_mm"], 1)

            def hidden(b, hf, k, bank):
                for c in range(DC):
                    last = mm(spare(bank), wf1[:, c, k * P:(k + 1) * P], nt[:, c, hf * HALF:(hf + 1) * HALF],
                              start=(c == 0), stop=(c == DC - 1))
                last.then_inc(S["ff_mm"], 1)

            def partial_logits(b, hf, bank):
                wait(pe, "ff_act", b * 16 + 8 * hf + 8)
                for k in range(HC):
                    cg = 32 * (k % 4)
                    last = mm(spare(bank)[cg:cg + 32, :], wr[:, k, :], ht[:, k, :], start=(k < 4), stop=(k >= 4))
                last.then_inc(S["lg_mm"], 1)

            def turn_logits(b, hf, bank):
                wait(pe, "lt_ready", b * 2 + hf + 1)
                for t in range(4):
                    last = mm(spare(bank)[:, t * EXPERTS:(t + 1) * EXPERTS], lt[:, t * P:(t + 1) * P], pick[:],
                              start=True, stop=True)
                last.then_inc(S["lg2_mm"], 1)

            def router(b):
                for k in range(HC):
                    if k == 0:
                        wait(pe, "xt_read", b * 4 + 4)
                    if k >= 2:
                        wait(pe, "ff_act", b * 16 + k - 1)
                    hidden(b, 0, k, k)
                partial_logits(b, 0, 0)
                hidden(b, 1, 0, 1)
                turn_logits(b, 0, 0)
                for k in range(1, HC):
                    if k == 2:
                        wait(pe, "lg_done", b * 2 + 1)
                    else:
                        wait(pe, "ff_act", b * 16 + 8 + (k - 1 if k > 2 else 1))
                    hidden(b, 1, k, 1 if k == 1 else k)

            def front_start(b):
                for t in range(TILES):
                    for part in range(3):
                        embed(b, t, part)
                wait(pe, "emb_h", b * TILES + TILES)
                for j in range(8):
                    turn(b, j)
                wait(pe, "tr_read", b * 8 + 8)
                for j in range(4):
                    for c in range(DC):
                        project(b, 0, j, c)

            front_start(0)

            def image(b, par, before, after):
                values(b, 0)
                if before:
                    weigh(b - 1, 15, 0)
                    weigh(b - 1, 15, 1)
                values(b, 1)
                if before:
                    final(b - 1)
                for hf in range(2):
                    if before:
                        wait(pe, "fin_h", b * 4 - 1 + hf)
                    else:
                        wait(pe, "v_read", b * 4 + 3 + hf)
                    for c in range(DC):
                        gates(b, 0, hf, c)
                for k in range(STEPS):
                    if k == G_STEPS:
                        if after:
                            wait(pe, "emb_h", (b + 1) * TILES + TILES)
                        else:
                            wait(pe, "qk_lo", b * 8 + 8)
                        if before:
                            norm_turn(b - 1)
                        weigh(b, 7, 0)
                        weigh(b, 7, 1)
                        if before:
                            router(b - 1)
                    score(b, k)
                    if before and k == G_STEPS:
                        partial_logits(b - 1, 1, 0)
                    if before and k == G_STEPS + 1:
                        turn_logits(b - 1, 1, 1)
                    if k in QK1_AT:
                        j, c = QK1_AT[k]
                        if j < 2 and c == 0:
                            wait(pe, "g_exp", b * 4 + 1 + j)
                        project(b, 1, j, c)
                    if after and k in EMBED_AT:
                        t, part = EMBED_AT[k]
                        if t < 2 and part == 0:
                            wait(pe, "qk_lo", b * 8 + 7 + t)
                        embed(b + 1, t, part)
                    if k in GATE_AT:
                        hf, c = GATE_AT[k]
                        if before and hf == 0 and c == 0:
                            wait(pe, "lg_done", b * 2)
                        gates(b, 1, hf, c)
                    if after and k in TURN_AT:
                        if TURN_AT[k] < 2:
                            wait(pe, "g_exp", b * 4 + 3 + TURN_AT[k])
                        turn(b + 1, TURN_AT[k])
                    if after and k in QK0_AT:
                        j, c = QK0_AT[k]
                        if j == 0 and c == 0:
                            wait(pe, "tr_read", b * 8 + 16)
                        project(b + 1, 0, j, c)
                    if k in WEIGH_AT:
                        weigh(b, *WEIGH_AT[k])

            over_images(pe, image)
            weigh(IMAGES - 1, 15, 0)
            weigh(IMAGES - 1, 15, 1)
            final(IMAGES - 1)
            pe.wait_ge(S["fin_h"], IMAGES * 4)
            norm_turn(IMAGES - 1)
            router(IMAGES - 1)
            partial_logits(IMAGES - 1, 1, 0)
            turn_logits(IMAGES - 1, 1, 1)

            pe.wait_ge(S["r_oh"], 1)
            pe.wait_ge(S["c_consts"], 16 * 6)
            oh_flat = oh[:].rearrange("p t e -> p (t e)")
            mm(ps[:, 0, :], up[:], oh_flat, start=True, stop=True)
            mm(ps[:, 1, :], ones[:], oh_flat, start=True, stop=True).then_inc(S["r_mm"], 1)

            pe.wait_ge(S["slots_ready"], 1)
            pe.wait_ge(S["wd_in"], 16 * EXPERTS)

            def group_hidden(g, i):
                wait(pe, xg_in[i], g * 32 + 64 if i == 0 else g * 32 + 32)
                for c in range(DC):
                    wait(pe, "gt_read", g * 2 + c - 1)
                    for t in range(GROUP):
                        last = nc.tensor.transpose(ps[:, c, t * P:(t + 1) * P],
                                                   xg[:, i, t, c * P:(c + 1) * P], ident[:])
                    last.then_inc(S["gt_mm"], 1)
                wait(pe, "gt_read", g * 2 + 2)
                for k in range(HC):
                    wait(pe, "gf_act", g * 8 + k - 3)
                    for c in range(DC):
                        last = mm(ps[:, 2 + k % 4, :], wf1[:, c, k * P:(k + 1) * P], xgt[:, i, c, :],
                                  start=(c == 0), stop=(c == DC - 1))
                    last.then_inc(S["gf_mm"], 1)

            def group_rows(g, i):
                wait(pe, "gf_act", g * 8 + 8)
                for t in range(GROUP):
                    if t % 2 == 0:
                        wait(pe, "y_ready", g * 2 + t // 2 - 1)
                    e = pe.value_load(slot_expert[0:1, bass.ds(g * GROUP + t, 1)], min_val=0, max_val=EXPERTS - 1)
                    o = ps[:, 6 + t // 2, (t % 2) * D:(t % 2 + 1) * D]
                    for k in range(HC):
                        mm(o, hg[:, i, k, t * P:(t + 1) * P], wd[:, bass.ds(e, 1), k, :],
                           start=(k == 0), stop=False, skip_group_check=True)
                    last = mm(o, ones[0:1, :], bd[0:1, bass.ds(e, 1), :], start=False, stop=True, skip_group_check=True)
                    if t % 2:
                        last.then_inc(S["y_mm"], 1)

            group_hidden(0, 0)
            group_hidden(1, 1)
            group_rows(0, 0)
            with pe.Fori(1, SORT_GROUPS // 2) as j:
                group_hidden(j * 2, 0)
                group_rows(j * 2 - 1, 1)
                group_hidden(j * 2 + 1, 1)
                group_rows(j * 2, 0)
            group_rows(SORT_GROUPS - 1, 1)

        @block.scalar
        def _(act):
            actv = nc.scalar.activation

            def spare(j):
                return ps[:, SPARE + j % 2, :]

            for j in range(4):
                act.wait_ge(S["pos_mm"], j + 1)
                actv(posr[:, j // 2, (j % 2) * HALF:(j % 2 + 1) * HALF], ps[:, j, :], ACT.Relu).then_inc(S["pos_relu"], 1)
            for j in range(4):
                act.wait_ge(S["pos_mm2"], 2 * j + 2)
                actv(posb[:, 2 * j:2 * j + 2, :].rearrange("p t d -> p (t d)"), ps[:, 4 + j, :], ACT.Identity
                     ).then_inc(S["pos_done"], 1)

            def turned(b, j):
                hf, w = j // 4, j % 4
                wait(act, "tr_mm", b * 8 + j + 1)
                if w < 2:
                    actv(nt[:, w, hf * HALF:(hf + 1) * HALF], spare(j), ACT.Identity,
                         bias=beta[:, w:w + 1], scale=gamma[:, w:w + 1]).then_inc(S["tr_read"], 1)
                else:
                    actv(at[:, w - 2, hf * HALF:(hf + 1) * HALF], spare(j), ACT.Identity).then_inc(S["tr_read"], 1)

            def high(b, g, j):
                hf, w = j // 2, j % 2
                wait(act, "qk_mm", b * 8 + 4 * g + j + 1)
                if j == 0:
                    if g == 0:
                        wait(act, stacked[1], b * 24 * 16)
                    else:
                        wait(act, stacked[0], (b * 24 + 24) * 16)
                actv(qk[:, w, 0, hf * HALF:(hf + 1) * HALF], spare(j), ACT.Identity,
                     scale=(SCALE if w == 0 else 1.0)).then_inc(S["qk_hi"], 1)

            def gated_exp(b, c, hf):
                wait(act, "g_mm", b * 4 + 2 * c + hf + 1)
                actv(gate[:, c, hf * HALF:(hf + 1) * HALF], spare(hf), ACT.Exp,
                     bias=nbgate[:, c:c + 1], scale=-1.0).then_inc(S["g_exp"], 1)

            def router(b):
                for j in range(4):
                    wait(act, "xt_mm", b * 4 + j + 1)
                    actv(nt[:, j % 2, (j // 2) * HALF:(j // 2 + 1) * HALF], spare(j), ACT.Identity).then_inc(S["xt_read"], 1)
                for hf in range(2):
                    for k in range(HC):
                        bank = 1 if hf == 1 and k == 0 else k
                        wait(act, "ff_mm", b * 16 + 8 * hf + k + 1)
                        if hf == 1:
                            wait(act, "lg_mm", b * 2 + 1)
                        actv(ht[:, k, :], spare(bank), ACT.Gelu, bias=bf1[:, k:k + 1]).then_inc(S["ff_act"], 1)

            for j in range(8):
                turned(0, j)
            for j in range(4):
                high(0, 0, j)

            def image(b, par, before, after):
                for j in range(4):
                    wait(act, "v_mm", b * 4 + j + 1)
                    wait(act, "vs_ready", b * 16)
                    actv(v[:, 2 * j:2 * j + 2, :].rearrange("p t d -> p (t d)"), spare(j), ACT.Identity
                         ).then_inc(S["v_read"], 1)
                if before:
                    wait(act, "fin_mm", b * 4)
                for hf in range(2):
                    gated_exp(b, 0, hf)
                for k in range(STEPS):
                    if k == G_STEPS and before:
                        router(b - 1)
                    wait(act, "max_done", b * STEPS + k + 1)
                    if k >= PR:
                        wait(act, "pv_mm", b * 16 + (k - PR) // 4 + 1)
                    actv(pr[:, k % PR, :], ps[:, 2 * (k % SR):2 * (k % SR) + 2, :].rearrange("p a n -> p (a n)"),
                         ACT.Exp, bias=nmax[:, k % 16:k % 16 + 1], accum_out=rsum[:, k % 16:k % 16 + 1]
                         ).then_inc(S["exp_done"], 1)
                    if after and k in TURN_AT:
                        turned(b + 1, TURN_AT[k])
                    if k in QK1_AT and QK1_AT[k][1] == 1:
                        high(b, 1, QK1_AT[k][0])
                    if k in GATE_AT and GATE_AT[k][1] == 1:
                        gated_exp(b, 1, GATE_AT[k][0])
                    if after and k in QK0_AT and QK0_AT[k][1] == 1:
                        high(b + 1, 0, QK0_AT[k][0])

            over_images(act, image)
            router(IMAGES - 1)
            act.wait_ge(S["r_exp"], 1)
            actv(ee[:], ee[:], ACT.Exp).then_inc(S["r_exp"], 1)

            def group_hidden(g, i):
                for k in range(HC):
                    wait(act, "gf_mm", g * 8 + k + 1)
                    if k == 0:
                        wait(act, "y_mm", g * 2 - 2)
                    actv(hg[:, i, k, :], ps[:, 2 + k % 4, :], ACT.Gelu, bias=bf1[:, k:k + 1]).then_inc(S["gf_act"], 1)

            over_groups(act, group_hidden)

        @block.vector
        def _(dve):
            V = nc.vector

            def spare(j):
                return ps[:, SPARE + j % 2, :]

            V.memset(ones[:], 1.0).then_inc(S["setup"], 1)
            dve.wait_ge(S["consts"], 16 * N_CONSTS)
            V.tensor_scalar(nbgate[:], bgate, -1.0, None, ALU.mult).then_inc(S["setup"], 1)
            dve.wait_ge(S["setup"], 2)

            def stats(src, b, ln):
                for t in range(TILES):
                    last = V.bn_stats(bst[:, ln - 1, t, :], src[:, t, :])
                last.then_inc(S[f"stats{ln}"], 1)
                hold(dve, f"stats{ln}", b + 1)
                for t in range(TILES):
                    last = V.bn_aggr(mv[:, ln - 1, t, :], bst[:, ln - 1, t, :])
                last.then_inc(S[f"var{ln}"], 1)

            def normalise(dst, src, b, ln, done):
                hold(dve, f"rstd{ln}", b + 1)
                for t in range(TILES):
                    last = V.tensor_scalar(dst[:, t, :], src[:, t, :], mv[:, ln - 1, t, 0:1],
                                           rstd[:, ln - 1, t:t + 1], ALU.subtract, ALU.mult)
                last.then_inc(S[done], 1)

            def embedded(b, par, t):
                wait(dve, "emb_mm", b * TILES + t + 1)
                if t == 0:
                    wait(dve, "h_out", b * 16 - 16)
                V.tensor_tensor(hres[:, par, t, :], spare(t)[:, 0:D], posb[:, t, :], ALU.add).then_inc(S["emb_h"], 1)

            def norm_1(b, par):
                wait(dve, "emb_h", b * TILES + TILES)
                stats(hres[:, par], b, 1)
                normalise(a, hres[:, par], b, 1, "a_ready")

            def stats_2(b):
                wait(dve, "a_ready", b + 1)
                stats(a, b, 2)

            def norm_2(b, before):
                if before:
                    wait(dve, "xn_out", b * 16 - 16)
                    wait(dve, "xt_mm", b * 4 - 4)
                normalise(n, a, b, 2, "n_ready")

            def low(b, g, j):
                hf, w = j // 2, j % 2
                wait(dve, "qk_hi", b * 8 + 4 * g + j + 1)
                V.scalar_tensor_tensor(
                    qk[:, w, 1, hf * HALF:(hf + 1) * HALF], spare(j), SCALE if w == 0 else 1.0,
                    qk[:, w, 0, hf * HALF:(hf + 1) * HALF].bitcast(F32), ALU.mult, ALU.subtract
                ).then_inc(S["qk_lo"], 1)

            def scale_v(b, gi):
                g, i = gi // TILES, gi % TILES
                col = (4 * gi) % 16
                wait(dve, "exp_done", b * STEPS + 4 * gi + 4)
                V.reciprocal(rinv[:, gi % 2, :], rsum[:, col:col + 4]).then_inc(S["rinv_done"], 1)
                wait(dve, "rinv_done", b * 16 + gi + 1)
                wait(dve, "pv_mm", b * 16 + gi - 1)
                V.tensor_tensor(vs[:, gi % 2], v[:, i, g * P:(g + 1) * P].rearrange("p (a d) -> p a d", a=4),
                                rinv[:, gi % 2, :, None].broadcast_to([P, 4, HD]), ALU.mult).then_inc(S["vs_ready"], 1)

            def invert(b, c, q):
                if q % 4 == 0:
                    wait(dve, "g_one", b * 4 + 2 * c + q // 4 + 1)
                piece = gate[:, c, q * P:(q + 1) * P]
                V.reciprocal(piece, piece).then_inc(S["g_ready"], 1)

            def gated(b, g):
                wait(dve, "pv_mm", b * 16 + 8 * (g + 1))
                wait(dve, "g_ready", b * 16 + 8 * (g + 1))
                for j in range(2):
                    piece = gate[:, g, j * 512:(j + 1) * 512]
                    V.tensor_tensor(piece, ps[:, O_BANK + j, :], piece, ALU.mult).then_inc(S["og_ready"], 1)

            def added(b, par):
                h = hres[:, par].rearrange("p t d -> p (t d)")
                wait(dve, "ha_ready", b + 1)
                for j in range(4):
                    wait(dve, "fin_mm", b * 4 + j + 1)
                    V.tensor_tensor(h[:, j * 512:(j + 1) * 512], h[:, j * 512:(j + 1) * 512], spare(j), ALU.add
                                    ).then_inc(S["fin_h"], 1)

            def stats_3(b, par):
                wait(dve, "fin_h", b * 4 + 4)
                stats(hres[:, par], b, 3)

            def norm_3(b, par, t):
                if t == 0:
                    wait(dve, "tr_mm", b * 8 + 16 if not isinstance(b, int) or b < IMAGES - 1 else b * 8 + 8)
                    hold(dve, "rstd3", b + 1)
                last = V.tensor_scalar(n[:, t, :], hres[:, par, t, :], mv[:, 2, t, 0:1], rstd[:, 2, t:t + 1],
                                       ALU.subtract, ALU.mult)
                if t == TILES - 1:
                    last.then_inc(S["xn_ready"], 1)

            def logit_sums(b, hf):
                wait(dve, "lg_mm", b * 2 + hf + 1)
                if hf == 1:
                    wait(dve, "lg2_mm", b * 2 + 1)
                V.tensor_copy(lt[:], spare(0)).then_inc(S["lt_ready"], 1)

            def keep_logits(b, hf):
                wait(dve, "lg2_mm", b * 2 + hf + 1)
                V.tensor_copy(logits[:, bass.ds(b * TILES + 4 * hf, 4), :],
                              spare(hf)[:, 0:4 * EXPERTS].rearrange("p (t e) -> p t e", e=EXPERTS)
                              ).then_inc(S["lg_done"], 1)

            for t in range(TILES):
                embedded(0, 0, t)
            norm_1(0, 0)
            stats_2(0)
            norm_2(0, False)
            for j in range(4):
                low(0, 0, j)

            def image(b, par, before, after):
                if before:
                    scale_v(b - 1, 15)
                    gated(b - 1, 1)
                    added(b - 1, 1 - par)
                    stats_3(b - 1, 1 - par)
                for k in range(STEPS):
                    if k == G_STEPS:
                        scale_v(b, 7)
                        if after:
                            norm_1(b + 1, 1 - par)
                            stats_2(b + 1)
                            norm_2(b + 1, before)
                        for q in range(8):
                            invert(b, 0, q)
                        gated(b, 0)
                        if before:
                            logit_sums(b - 1, 0)
                            keep_logits(b - 1, 0)
                    wait(dve, "score_mm", b * STEPS + k + 1)
                    V.reduce_max(nmax[:, k % 16:k % 16 + 1],
                                 ps[:, 2 * (k % SR):2 * (k % SR) + 2, :].rearrange("p a n -> p (a n)"),
                                 AX_X, negate=True).then_inc(S["max_done"], 1)
                    if before and k == G_STEPS:
                        logit_sums(b - 1, 1)
                    if before and k == G_STEPS + 1:
                        keep_logits(b - 1, 1)
                    if k in SCALE_AT:
                        scale_v(b, SCALE_AT[k])
                    if before and k in NORM_AT:
                        norm_3(b - 1, 1 - par, NORM_AT[k])
                    if k in INVERT_AT:
                        invert(b, 1, INVERT_AT[k])
                    if k in LOW1_AT:
                        low(b, 1, LOW1_AT[k])
                    if after and k in EMBED_AT and EMBED_AT[k][1] == 2:
                        embedded(b + 1, 1 - par, EMBED_AT[k][0])
                    if after and k in LOW0_AT:
                        low(b + 1, 0, LOW0_AT[k])

            over_images(dve, image)
            last_b, last_par = IMAGES - 1, (IMAGES - 1) % 2
            scale_v(last_b, 15)
            gated(last_b, 1)
            added(last_b, last_par)
            stats_3(last_b, last_par)
            dve.wait_ge(S["xn_out"], 16 * last_b)
            for t in range(TILES):
                norm_3(last_b, last_par, t)
            for hf in range(2):
                logit_sums(last_b, hf)
                keep_logits(last_b, hf)

            links = [0]

            def link(ins):
                links[0] += 1
                ins.then_inc(S["chain"], 1)
                dve.wait_ge(S["chain"], links[0])

            wide = [P, ALL_TILES, EXPERTS]
            dve.wait_ge(S["lg_done"], 2 * IMAGES)
            dve.wait_ge(S["c_consts"], 16 * 6)
            link(V.tensor_tensor(logits[:], logits[:], brt[:], ALU.add))
            link(V.reduce_max(red[:, 0, :], logits[:], AX_X))
            V.tensor_tensor(ee[:], logits[:], red[:, 0, :, None].broadcast_to(wide), ALU.subtract).then_inc(S["r_exp"], 1)
            link(V.memset(onesf[:], 1.0))
            dve.wait_ge(S["r_exp"], 2)
            link(V.reduce_max(red[:, 1, :], ee[:], AX_X))
            link(V.tensor_tensor(oh[:], ee[:], red[:, 1, :, None].broadcast_to(wide), ALU.is_ge))
            link(V.tensor_tensor(oh[:], oh[:], rnk[:], ALU.mult))
            link(V.reduce_max(red[:, 3, :], oh[:], AX_X))
            V.tensor_tensor(oh[:], oh[:], red[:, 3, :, None].broadcast_to(wide), ALU.is_equal).then_inc(S["r_oh"], 1)
            dve.wait_ge(S["r_mm"], 1)
            link(V.tensor_copy(tot[:].rearrange("p t e -> p (t e)"), ps[:, 1, :]))
            for e in range(EXPERTS):
                V.tensor_tensor_scan(run[:, :, e], onesf[:], tot[:, :, e], 0.0, ALU.mult, ALU.add)
            link(V.memset(slot_f[:], 0.0))
            link(V.tensor_scalar(cnt_i[:, 0, :], run[:, ALL_TILES - 1, :], float(P - 1), None, ALU.add))
            link(V.tensor_scalar(cnt_i[:, 1, :], cnt_i[:, 0, :], 7, 7, ALU.arith_shift_right, ALU.logical_shift_left))
            link(V.tensor_copy(cnt[:, 0, :], cnt_i[:, 1, :]))
            link(V.tensor_tensor_scan(cnt[:, 1, :], onesf[:, 0:EXPERTS], cnt[:, 0, :], 0.0, ALU.mult, ALU.add))
            link(V.tensor_tensor(cnt[:, 2, :], cnt[:, 1, :], cnt[:, 0, :], ALU.subtract))
            link(V.tensor_tensor(run[:], run[:], tot[:], ALU.subtract))
            link(V.tensor_tensor(run[:].rearrange("p t e -> p (t e)"), run[:].rearrange("p t e -> p (t e)"), ps[:, 0, :], ALU.add))
            link(V.tensor_tensor(run[:], run[:], cnt[:, 2, None, :].broadcast_to(wide), ALU.add))
            link(V.tensor_tensor(run[:], run[:], oh[:], ALU.mult))
            link(V.reduce_sum(place_f[:], run[:], AX_X))
            link(V.tensor_copy(place_i[:], place_f[:]))
            link(V.tensor_scalar(place_a[:, 0, :], place_i[:], P - 1, None, ALU.bitwise_and))
            link(V.tensor_scalar(place_a[:, 1, :], place_i[:], 7, None, ALU.arith_shift_right))
            link(V.scalar_tensor_tensor(place_a[:, 2, :], place_a[:, 0, :], float(SLOTS), place_a[:, 1, :], ALU.mult, ALU.add))

            def stage_ids(j):
                for i in range(2):
                    wait(dve, inv_out[i], j * 128)
                    V.tensor_copy(inv_tok[:, i], tid[:, bass.ds(j * 16 + 8 * i, 8)])
                    V.tensor_copy(inv_pos[:, i], place_a[:, 2, bass.ds(j * 16 + 8 * i, 8)]).then_inc(S["inv_stage"], 1)

            over_pairs(dve, ALL_TILES // 16, stage_ids)
            for e in range(EXPERTS):
                link(V.scalar_tensor_tensor(slot_f[:, (e + 1) % 2, :], sst[:], cnt[:, 1, e:e + 1], slot_f[:, e % 2, :],
                                            ALU.is_ge, ALU.add))
            V.tensor_scalar(slot_expert[:], slot_f[:, EXPERTS % 2, :], float(EXPERTS - 1), None, ALU.min).then_inc(S["slots_ready"], 1)
            link(V.reduce_sum(red[:, 2, :], ee[:], AX_X))
            link(V.reciprocal(red[:, 2, :], red[:, 2, :]))
            link(V.tensor_tensor(prob[:], red[:, 1, :], red[:, 2, :], ALU.mult))

            def turned_rows(g, i):
                for c in range(DC):
                    wait(dve, "gt_mm", g * 2 + c + 1)
                    V.tensor_copy(xgt[:, i, c, :], ps[:, c, :]).then_inc(S["gt_read"], 1)

            def expert_rows(g, i):
                wait(dve, y_out[i], g * 8 if i == 0 else g * 8 - 8)
                for j in range(2):
                    wait(dve, "y_mm", g * 2 + j + 1)
                    V.tensor_copy(yo[:, i, 2 * j:2 * j + 2, :].rearrange("p t d -> p (t d)"), ps[:, 6 + j, :]
                                  ).then_inc(S["y_ready"], 1)

            turned_rows(0, 0)
            turned_rows(1, 1)
            expert_rows(0, 0)
            with dve.Fori(1, SORT_GROUPS // 2) as j:
                turned_rows(j * 2, 0)
                expert_rows(j * 2 - 1, 1)
                turned_rows(j * 2 + 1, 1)
                expert_rows(j * 2, 0)
            expert_rows(SORT_GROUPS - 1, 1)

            def finish(j):
                for i in range(2):
                    V.tensor_copy(pcol[:, i], prob[:, bass.ds(j * 16 + 8 * i, 8)]).then_inc(S["pcol_ready"], 1)
                    wait(dve, "pcol_ready", j * 2 + i + 1)
                    wait(dve, yg_in[i], j * 128 + 128)
                    wait(dve, hr_in[i], j * 16 + 16)
                    for k in range(8):
                        last = V.scalar_tensor_tensor(yg[:, i, k, :], yg[:, i, k, :], pcol[:, i, k:k + 1], hr[:, i, k, :],
                                                      ALU.mult, ALU.add)
                    last.then_inc(S["o_ready"], 1)

            over_pairs(dve, IMAGES // 2, finish)


def kernel(**inputs):
    import numpy as np
    import concourse.bacc as bacc
    from concourse.bass_utils import run_bass_kernel_spmd

    c = np.ascontiguousarray

    def chunked(w):
        return c(w.reshape(-1, P, w.shape[-1]).transpose(1, 0, 2))

    a = {k: np.asarray(v) for k, v in inputs.items()}
    x = a["x"].reshape(IMAGES, 3, 32, 16, 32, 16).transpose(0, 1, 3, 5, 2, 4).reshape(IMAGES, KC, P, TILES, P)
    x = c(x.transpose(0, 3, 2, 1, 4))
    f32 = np.float32
    grid = np.arange(32, dtype=f32) / f32(31)
    pos_in = np.stack([np.repeat(grid, 32), np.tile(grid, 32), np.ones(TOKENS, f32)])
    w_qkv = a["L0_attn_W_qkv"].T
    router = np.concatenate([a["L0_ffn_Wg"], np.zeros((HID, 32 - EXPERTS), f32)], 1)
    pick = np.tile(np.concatenate([np.eye(EXPERTS, dtype=f32), np.zeros((32 - EXPERTS, EXPERTS), f32)]), (4, 1))
    rank = np.tile((EXPERTS - np.arange(EXPERTS, dtype=f32)), (P, ALL_TILES, 1))
    rank = np.concatenate([rank, np.repeat(pick[:, None, :], ALL_TILES, 1)], 2)
    tid = (np.arange(ALL_TILES)[None, :] * P + np.arange(P)[:, None]).astype(np.int32)
    tid = np.concatenate([tid, np.zeros((P, SLOTS), np.int32)], 1)
    arrays = {
        "x_in": x,
        "w_patch": chunked(a["L0_tok_Wp"]),
        "pos_in": c(pos_in),
        "pos_w1": c(np.concatenate([a["L0_tok_W1"], a["L0_tok_b1"][None]], 0)),
        "pos_w2": chunked(a["L0_tok_W2"]),
        "pos_bias": c(np.stack([a["L0_tok_b2"], a["L0_tok_bp"]])),
        "ln_gamma": c(a["L0_attn_ln_gamma"].reshape(DC, P).T),
        "ln_beta": c(a["L0_attn_ln_beta"].reshape(DC, P).T),
        "w_qk": chunked(w_qkv[:, :2 * D]),
        "w_v": chunked(w_qkv[:, 2 * D:]),
        "w_gate": chunked(a["L0_attn_W_gate"].T),
        "b_gate": c(a["L0_attn_b_gate"].reshape(DC, P).T),
        "w_final": chunked(a["L0_attn_W_final"].T),
        "b_final": c(np.tile(a["L0_attn_b_final"], (P, 1))),
        "w_ffn1": chunked(a["L0_ffn_W1"]),
        "b_ffn1": c(a["L0_ffn_b1"].reshape(HC, P).T),
        "w_router": chunked(router),
        "b_router": c(np.tile(a["L0_ffn_bg"], (P, ALL_TILES, 1))),
        "w_down": c(a["L0_ffn_Wd"].reshape(EXPERTS, HC, P, D).transpose(0, 2, 1, 3)),
        "b_down": c(a["L0_ffn_bd"][None]),
        "identity": np.eye(P, dtype=f32),
        "upper": np.triu(np.ones((P, P), f32), 1),
        "rank": c(rank),
        "slot_start": c(np.tile(np.arange(SLOTS, dtype=f32) * P, (P, 1))),
        "token_id": c(tid),
    }
    nc = bacc.Bacc("TRN2", target_bir_lowering=False, num_devices=1)
    aps = [nc.dram_tensor(k, v.shape, mybir.dt.from_np(v.dtype), kind="ExternalInput").ap() for k, v in arrays.items()]
    aps.append(nc.dram_tensor("out", (IMAGES, TOKENS, D), F32, kind="ExternalOutput").ap())
    vit_layer_kernel(nc, *aps)
    r = run_bass_kernel_spmd(nc, [arrays], core_ids=[0])
    return r.results[0]["out"]
```

```python
from contextlib import ExitStack

import concourse.bass as bass
from concourse import mybir

F32 = mybir.dt.float32
F32R = mybir.dt.float32r
I32 = mybir.dt.int32
ALU = mybir.AluOpType
ACT = mybir.ActivationFunctionType
AX_X = mybir.AxisListType.X

P = 128
IMAGES = 8
TOKENS = 1024
TILES = TOKENS // P
ALL_TILES = IMAGES * TILES
D = 256
DC = D // P
KC = 3 * 16 * 16 // P
HALF = TOKENS // 2
HEADS, HD = 8, 32
GROUPS = HEADS // 4
STEPS = HEADS * TILES
HID = 1024
HC = HID // P
EXPERTS = 8
SLOTS = ALL_TILES + EXPERTS
GROUP = 2
SORT_GROUPS = SLOTS // GROUP
WD_BUFFERS = 4
WD_PIECES = 2 * EXPERTS
G_STEPS = STEPS // GROUPS
PR = 8
SR = 2
O_BANK, SPARE = 4, 6
EPS = 1e-5
SCALE = float(HD) ** -0.5


def vit_layer_kernel(nc, x, w_patch, pos_in, pos_w1, pos_w2, pos_bias, ln_gamma, ln_beta, w_qk, w_v,
                     w_gate, b_gate, w_final, b_final, w_ffn1, b_ffn1, w_router, b_router, w_down,
                     b_down, identity, pick_in, upper, rank, slot_start, column, token_id, out):
    xn_rows = nc.dram_tensor("xn_rows", (ALL_TILES * P, D), F32).ap()
    h_rows = nc.dram_tensor("h_rows", (ALL_TILES * P, D), F32).ap()

    h_view = h_rows.rearrange("(b t p) d -> b p t d", b=IMAGES, t=TILES)
    xn_view = xn_rows.rearrange("(b t p) d -> b p t d", b=IMAGES, t=TILES)
    out_rows = out.rearrange("b t d -> (b t) d")

    with ExitStack() as ctx:
        def sem(name):
            return ctx.enter_context(nc.semaphore(name))

        def tensor(stack, name, shape, dt=F32):
            return stack.enter_context(nc.sbuf_tensor(name, shape, dt))

        ps = ctx.enter_context(nc.psum_tensor("ps", [P, 8, 512], F32))

        ident = tensor(ctx, "ident", [P, P])
        wf1 = tensor(ctx, "wf1", [P, 2, DC, HID], F32R)
        bf1 = tensor(ctx, "bf1", [P, HC])
        ones = tensor(ctx, "ones", [P, P], F32R)
        logits = tensor(ctx, "logits", [P, ALL_TILES, EXPERTS])
        up = tensor(ctx, "up", [P, P])
        rnk = tensor(ctx, "rnk", [P, EXPERTS])
        brt = tensor(ctx, "brt", [P, EXPERTS])
        sst = tensor(ctx, "sst", [P, SLOTS])
        tid = tensor(ctx, "tid", [P, ALL_TILES])
        col = tensor(ctx, "col", [P, P])

        sa = ExitStack()
        wp = tensor(sa, "wp", [P, KC, D])
        wqk = tensor(sa, "wqk", [P, DC, 2 * D])
        wv = tensor(sa, "wv", [P, DC, D])
        wg = tensor(sa, "wg", [P, DC, D])
        wfin = tensor(sa, "wfin", [P, DC, D])
        wr = tensor(sa, "wr", [P, HC, 32])
        posb = tensor(sa, "posb", [P, TILES, D])
        vecs = tensor(sa, "vecs", [P, 3, DC])
        gamma, beta, bgate = vecs[:, 0, :], vecs[:, 1, :], vecs[:, 2, :]
        nbgate = tensor(sa, "nbgate", [P, DC])
        bfin = tensor(sa, "bfin", [P, D])
        pick = tensor(sa, "pick", [P, EXPERTS])
        xt = tensor(sa, "xt", [P, 2, KC, P])
        hres = tensor(sa, "hres", [P, 2, TILES, D])
        a = tensor(sa, "a", [P, TILES, D])
        n = tensor(sa, "n", [P, TILES, D])
        at = tensor(sa, "at", [P, DC, TOKENS])
        qk = tensor(sa, "qk", [P, 2, 2, TOKENS], F32R)
        stq = tensor(sa, "stq", [96, 4, TOKENS], F32R)
        stk = tensor(sa, "stk", [96, 4, TOKENS], F32R)
        v = tensor(sa, "v", [P, TILES, D])
        vs = tensor(sa, "vs", [P, 2, 4, HD])
        bst = tensor(sa, "bst", [P, 3, TILES, 6])
        mv = tensor(sa, "mv", [P, 3, TILES, 2])
        rstd = tensor(sa, "rstd", [P, 3, TILES])
        vare = tensor(sa, "vare", [P, 3, TILES])
        half_neg = tensor(sa, "half_neg", [P, TILES])
        nmax = tensor(sa, "nmax", [P, 16])
        rsum = tensor(sa, "rsum", [P, 16])
        rinv = tensor(sa, "rinv", [P, 2, 4])
        gate = tensor(sa, "gate", [P, DC, TOKENS])
        turned = ExitStack()
        nt = tensor(turned, "nt", [P, DC, TOKENS])
        pr = tensor(turned, "pr", [P, PR, TOKENS])
        turned.close()
        rear = ExitStack()
        nt_high = tensor(rear, "nt_high", [P, DC, TOKENS], F32R)
        nt_low = tensor(rear, "nt_low", [P, DC, TOKENS], F32R)
        lt = tensor(rear, "lt", [P, 4, HALF])[:, 0, :]
        ht = tensor(rear, "ht", [P, HC, HALF])
        rear.close()
        posin = pr[0:3, 0, :]
        posw1 = pr[0:3, 1, 0:D]
        sa.close()

        sc = ExitStack()
        slot_prob = tensor(sc, "slot_prob", [P, SLOTS])
        slot_from = tensor(sc, "slot_from", [P, SLOTS], I32)
        slot_to = tensor(sc, "slot_to", [P, SLOTS], I32)
        slot_expert = tensor(sc, "slot_expert", [P, SLOTS], I32)
        wd = tensor(sc, "wd", [P, 2, EXPERTS, HC, D], F32R)
        bd = tensor(sc, "bd", [2, EXPERTS, D], F32R)
        sb = ExitStack()
        prob = tensor(sb, "prob", [P, ALL_TILES])
        place_i = tensor(sb, "place_i", [P, ALL_TILES], I32)
        low_f = tensor(sb, "low_f", [P, ALL_TILES])
        high_f = tensor(sb, "high_f", [P, ALL_TILES])
        row_hot = tensor(sb, "row_hot", [P, 2, 8, P])
        slot_val = tensor(sb, "slot_val", [P, 2, 8, 2, SLOTS])
        ee = tensor(sb, "ee", [P, ALL_TILES, EXPERTS])
        oh = tensor(sb, "oh", [P, ALL_TILES, EXPERTS])
        tot = tensor(sb, "tot", [P, ALL_TILES, EXPERTS])
        run = tensor(sb, "run", [P, ALL_TILES, EXPERTS])
        red = tensor(sb, "red", [P, 4, ALL_TILES])
        onesf = tensor(sb, "onesf", [P, ALL_TILES])
        cnt_i = tensor(sb, "cnt_i", [P, 2, EXPERTS], I32)
        cnt = tensor(sb, "cnt", [P, 3, EXPERTS])
        slot_f = tensor(sb, "slot_f", [P, 2, SLOTS])
        place_f = tensor(sb, "place_f", [P, ALL_TILES])
        low_i = tensor(sb, "low_i", [P, ALL_TILES], I32)
        bd_raw = tensor(sb, "bd_raw", [EXPERTS, D])
        bd_parts = tensor(sb, "bd_parts", [EXPERTS, 2, D], F32R)
        wd_raw = tensor(sb, "wd_raw", [P, WD_BUFFERS, HC // 2, D])
        sb.close()
        idx = tensor(sc, "idx", [P, 2, GROUP], I32)
        xg = tensor(sc, "xg", [P, 2, GROUP, D])
        xgt = tensor(sc, "xgt", [P, 2, 2, DC, GROUP * P], F32R)
        hraw = tensor(sc, "hraw", [P, 2, GROUP * P])
        hg = tensor(sc, "hg", [P, 2, 2, HC, GROUP * P], F32R)
        back = tensor(sc, "back", [P, 2, GROUP], I32)
        pcol = tensor(sc, "pcol", [P, 2, GROUP])
        hr = tensor(sc, "hr", [P, 2, GROUP, D])
        sc.close()

        S = {}
        for name in ("consts setup pos_in pos_mm pos_relu pos_mm2 pos_done x_in0 x_in1 emb_mm emb_h "
                     "stats1 stats2 stats3 var1 var2 var3 eps1 eps2 eps3 rstd1 rstd2 rstd3 pow_ready "
                     "a_ready n_ready xn_ready tr_mm tr_read h_sum ha_ready qk_mm qk_hi qk_lo v_mm v_read "
                     "g_mm g_exp g_one g_ready stack0 stack1 score_mm max_done exp_done rinv_done vs_ready "
                     "pv_mm og_ready fin_mm fin_h h_out xn_out xt_mm xt_high xt_read ff_mm ff_act lg_mm lt_ready "
                     "lg2_mm lg_done bd_raw_in bd_high bd_low bd_in wd_in0 wd_in1 wd_in2 wd_in3 wd_high "
                     "wd_low chain r_exp r_oh r_mm slots_ready hot_ready val_ready sort_mm "
                     "idx_ready xg_in0 xg_in1 gt_mm gt_high gt_read wf1_high gf_mm gf_act hid_high hid_low "
                     "y_mm y_ready y_out0 y_out1 slots_in back_idx hr_in0 hr_in1 pcol_ready").split():
            S[name] = sem(name)

        def both(name):
            return S[name + "0"], S[name + "1"]

        x_in, stacked = both("x_in"), both("stack")
        xg_in, y_out, hr_in = (both(k) for k in ("xg_in", "y_out", "hr_in"))
        wd_in = [S[f"wd_in{i}"] for i in range(WD_BUFFERS)]
        FULL = 16 * GROUP

        def wd_piece(part, m):
            return wd[:, part].rearrange("p e k d -> p (e k) d")[:, bass.ds(m * (HC // 2), HC // 2), :]

        posr = nt
        posw2 = at[:, 0, 0:DC * D].rearrange("p (c d) -> p c d", c=DC)
        posbias = at[0:2, 1, 0:D]
        wf1_in = a[:].rearrange("p (c t) d -> p c (t d)", c=DC)
        N_CONSTS = 20

        def wait(eng, name, value):
            if not isinstance(value, int) or value > 0:
                eng.wait_ge(S[name] if isinstance(name, str) else name, value)

        def hold(eng, name, value):
            if not isinstance(value, int):
                value = eng.to_reg(value)
                eng.wait_ge(S["setup"], 1)
            wait(eng, name, value)

        def over_images(eng, body):
            body(0, 0, False, True)
            with eng.Fori(0, (IMAGES - 2) // 2) as j:
                body(j * 2 + 1, 1, True, True)
                body(j * 2 + 2, 0, True, True)
            body(IMAGES - 1, (IMAGES - 1) % 2, True, False)

        def over_groups(eng, body):
            body(0, 0)
            body(1, 1)
            with eng.Fori(1, SORT_GROUPS // 2) as j:
                body(j * 2, 0)
                body(j * 2 + 1, 1)

        def over_pairs(eng, count, body):
            body(0)
            with eng.Fori(1, count) as j:
                body(j)

        QK1_AT = {m: divmod(m, 2) for m in range(8)}
        EMBED_AT = {8 + m: divmod(m, 3) for m in range(24)}
        GATE_AT = {G_STEPS + 3 + m: divmod(m, 2) for m in range(4)}
        TURN_AT = {G_STEPS + 7 + j: j for j in range(8)}
        QK0_AT = {G_STEPS + 17 + 3 * j + c: (j, c) for j in range(4) for c in range(2)}
        LOW1_AT = {k + 2: j for k, (j, c) in QK1_AT.items() if c == 1}
        LOW0_AT = {k + 2: j for k, (j, c) in QK0_AT.items() if c == 1}
        NORM_AT = {2 + t: t for t in range(TILES)}
        INVERT_AT = {k: (0, q) for q, k in enumerate((11, 14, 17, 18, 21, 23, 26, 29))}
        INVERT_AT.update({G_STEPS + k: (1, q) for q, k in enumerate((10, 11, 13, 15, 17, 19, 22, 25))})
        SCALE_AT = {4 * i + 4: i for i in range(15) if i != 7}
        WEIGH_AT = {k: [(i, j) for i in range(15) if i != 7 for j in range(4)
                        if k == min(4 * i + 5 + j, (i // TILES + 1) * G_STEPS - 1)] for k in range(STEPS)}
        assert max(EMBED_AT) < G_STEPS and max(LOW0_AT) < STEPS

        block = ctx.enter_context(nc.Block())

        @block.sync
        def _(sp):
            for dst, src in ((posin, pos_in), (posw1, pos_w1), (posw2, pos_w2), (posbias, pos_bias)):
                sp.dma_start(dst, src).then_inc(S["pos_in"], 16)
            for dst, src in ((wp[:], w_patch), (ident[:], identity), (vecs[:, 0, :], ln_gamma),
                             (vecs[:, 1, :], ln_beta), (vecs[:, 2, :], b_gate), (wqk[:], w_qk), (wv[:], w_v),
                             (wg[:], w_gate), (wfin[:], w_final), (bfin[:], b_final), (wf1_in, w_ffn1),
                             (bf1[:], b_ffn1), (wr[:], w_router), (pick[:], pick_in), (up[:], upper),
                             (rnk[:], rank), (brt[:], b_router), (sst[:], slot_start), (tid[:], token_id),
                             (col[:], column)):
                sp.dma_start(dst, src).then_inc(S["consts"], 16)

            def load_tile(b, t):
                sp.dma_start(xt[:, t % 2], x[b, t]).then_inc(x_in[t % 2], 16)

            def load_rest(b):
                for t in range(2, TILES):
                    hold(sp, "emb_mm", b * TILES + t - 1)
                    load_tile(b, t)

            def load_stack(b, g):
                hold(sp, "qk_lo", b * 8 + 4 * (g + 1))
                hold(sp, "score_mm", b * STEPS + g * G_STEPS)
                for hh in range(4):
                    for r in range(3):
                        src = slice(32 * hh, 32 * hh + 32)
                        dst = slice(32 * r, 32 * r + 32)
                        sp.dma_start(stq[dst, hh, :].bitcast(F32), qk[src, 0, r % 2, :].bitcast(F32)
                                     ).then_inc(stacked[g], 16)
                        sp.dma_start(stk[dst, hh, :].bitcast(F32), qk[src, 1, r // 2, :].bitcast(F32)
                                     ).then_inc(stacked[g], 16)

            load_tile(0, 0)
            load_tile(0, 1)
            load_rest(0)

            def image(b, par, before, after):
                load_stack(b, 0)
                if after:
                    for t in range(2):
                        hold(sp, "emb_mm", b * TILES + 7 + t)
                        load_tile(b + 1, t)
                    load_rest(b + 1)
                load_stack(b, 1)

            over_images(sp, image)
            sp.wait_ge(S["lg_done"], 2 * IMAGES)
            sp.wait_ge(S["h_out"], 16 * IMAGES)
            sp.wait_ge(S["xn_out"], 16 * IMAGES)
            sp.dma_start(bd_raw[:], b_down).then_inc(S["bd_raw_in"], 16)

            def load_down(j):
                for i in range(WD_BUFFERS):
                    hold(sp, "wd_low", j * WD_BUFFERS + i + 1 - WD_BUFFERS)
                    sp.dma_start(wd_raw[:, i], w_down[j * WD_BUFFERS + i]).then_inc(wd_in[i], 16)

            over_pairs(sp, WD_PIECES // WD_BUFFERS, load_down)
            sp.wait_ge(S["bd_low"], 1)
            for part in range(2):
                for e in range(EXPERTS):
                    sp.dma_start(bd[part:part + 1, e, :].bitcast(F32), bd_parts[e:e + 1, part, :].bitcast(F32)
                                 ).then_inc(S["bd_in"], 16)
            for i in range(2):
                sp.wait_ge(y_out[i], 16 * GROUP * (SORT_GROUPS // 2))

        @block.gpsimd
        def _(pool):
            nc.gpsimd.memset(half_neg[:], -0.5).then_inc(S["pow_ready"], 1)
            pool.wait_ge(S["pow_ready"], 1)

            def root(ln, b):
                hold(pool, f"var{ln}", b + 1)
                nc.gpsimd.tensor_scalar(vare[:, ln - 1], mv[:, ln - 1, :, 1], EPS, None, ALU.add
                                        ).then_inc(S[f"eps{ln}"], 1)
                wait(pool, f"eps{ln}", b + 1)
                nc.gpsimd.tensor_tensor(rstd[:, ln - 1], vare[:, ln - 1], half_neg[:], ALU.pow
                                        ).then_inc(S[f"rstd{ln}"], 1)

            def front(b, par):
                root(1, b)
                root(2, b)
                h = hres[:, par]
                hold(pool, "n_ready", b + 1)
                nc.gpsimd.tensor_tensor(h, h, a[:], ALU.add).then_inc(S["h_sum"], 1)
                wait(pool, "h_sum", b + 1)
                nc.gpsimd.tensor_tensor(h, h, bfin[:, None, :].broadcast_to([P, TILES, D]), ALU.add
                                        ).then_inc(S["ha_ready"], 1)

            def add_one(b, c):
                for j in (2 * c, 2 * c + 1):
                    piece = gate[:, j // 2, (j % 2) * HALF:(j % 2 + 1) * HALF]
                    hold(pool, "g_exp", b * 4 + j + 1)
                    nc.gpsimd.tensor_scalar(piece, piece, 1.0, None, ALU.add).then_inc(S["g_one"], 1)

            def store_rear(b, par):
                hold(pool, "fin_h", b * 4 + 4)
                nc.gpsimd.dma_start(h_view[b], hres[:, par]).then_inc(S["h_out"], 16)
                hold(pool, "xn_ready", b + 1)
                nc.gpsimd.dma_start(xn_view[b], n[:]).then_inc(S["xn_out"], 16)

            front(0, 0)

            def image(b, par, before, after):
                if before:
                    root(3, b - 1)
                add_one(b, 0)
                if before:
                    store_rear(b - 1, 1 - par)
                if after:
                    front(b + 1, 1 - par)
                add_one(b, 1)

            over_images(pool, image)
            root(3, IMAGES - 1)
            store_rear(IMAGES - 1, (IMAGES - 1) % 2)

            pool.wait_ge(S["bd_high"], 1)
            nc.gpsimd.tensor_tensor(bd_parts[:, 1], bd_raw[:], bd_parts[:, 0].bitcast(F32), ALU.subtract
                                    ).then_inc(S["bd_low"], 1)

            def split_down(j):
                for i in range(WD_BUFFERS):
                    m = j * WD_BUFFERS + i
                    hold(pool, "wd_high", m + 1)
                    nc.gpsimd.tensor_tensor(wd_piece(1, m), wd_raw[:, i], wd_piece(0, m).bitcast(F32), ALU.subtract
                                            ).then_inc(S["wd_low"], 1)

            over_pairs(pool, WD_PIECES // WD_BUFFERS, split_down)
            pool.wait_ge(S["slots_in"], 1)
            pool.wait_ge(S["h_out"], 16 * IMAGES)
            pool.wait_ge(S["xn_out"], 16 * IMAGES)

            def gather_rows(g, i):
                hold(pool, "gt_mm", g * 2 - 2)
                hold(pool, hr_in[i], (g - i) * (FULL // 2))
                nc.gpsimd.tensor_copy(idx[:, i], slot_from[:, bass.ds(g * GROUP, GROUP)]).then_inc(S["idx_ready"], 1)
                hold(pool, "idx_ready", g + 1)
                for t in range(GROUP):
                    nc.gpsimd.indirect_dma_start(
                        xg[:, i, t, :], None, xn_rows,
                        bass.IndirectOffsetOnAxis(idx[:, i, t:t + 1], 0)).then_inc(xg_in[i], 16)

            def scatter_rows(g, i):
                hold(pool, "y_ready", g * 2 + 2)
                hold(pool, y_out[i], (g - i) * (FULL // 2))
                nc.gpsimd.tensor_copy(back[:, i], slot_to[:, bass.ds(g * GROUP, GROUP)]).then_inc(S["back_idx"], 1)
                hold(pool, "back_idx", g + 1)
                for t in range(GROUP):
                    nc.gpsimd.indirect_dma_start(
                        out_rows, bass.IndirectOffsetOnAxis(back[:, i, t:t + 1], 0), hr[:, i, t, :], None,
                        bounds_check=ALL_TILES * P - 1, oob_is_err=False).then_inc(y_out[i], 16)

            def gather_stream(g, i):
                hold(pool, y_out[i], (g - i) * (FULL // 2))
                for t in range(GROUP):
                    nc.gpsimd.indirect_dma_start(
                        hr[:, i, t, :], None, h_rows,
                        bass.IndirectOffsetOnAxis(idx[:, i, t:t + 1], 0)).then_inc(hr_in[i], 16)

            def turn(g, i):
                gather_rows(g + 1, 1 - i)
                scatter_rows(g - 2, i)
                gather_stream(g, i)

            gather_rows(0, 0)
            gather_stream(0, 0)
            gather_rows(1, 1)
            gather_stream(1, 1)
            gather_rows(2, 0)
            turn(2, 0)
            turn(3, 1)
            with pool.Fori(2, SORT_GROUPS // 2 - 1) as j:
                turn(j * 2, 0)
                turn(j * 2 + 1, 1)
            turn(SORT_GROUPS - 2, 0)
            scatter_rows(SORT_GROUPS - 3, 1)
            gather_stream(SORT_GROUPS - 1, 1)
            scatter_rows(SORT_GROUPS - 2, 0)
            scatter_rows(SORT_GROUPS - 1, 1)

        @block.tensor
        def _(pe):
            mm = nc.tensor.matmul

            def spare(j):
                return ps[:, SPARE + j % 2, :]

            pe.wait_ge(S["pos_in"], 16 * 4)
            for c in range(DC):
                for hf in range(2):
                    mm(ps[:, 2 * c + hf, :], posw1[:, c * P:(c + 1) * P], posin[:, hf * HALF:(hf + 1) * HALF],
                       start=True, stop=True).then_inc(S["pos_mm"], 1)
            pe.wait_ge(S["pos_relu"], 4)
            pe.wait_ge(S["setup"], 1)
            for t in range(TILES):
                o = ps[:, 4 + t // 2, (t % 2) * D:(t % 2 + 1) * D]
                for c in range(DC):
                    mm(o, posr[:, c, t * P:(t + 1) * P], posw2[:, c, :], start=(c == 0), stop=False, skip_group_check=True)
                mm(o, ones[0:2, :].bitcast(F32), posbias, start=False, stop=True, skip_group_check=True).then_inc(S["pos_mm2"], 1)
            pe.wait_ge(S["pos_done"], 4)

            def embed(b, t, part):
                if part == 0:
                    wait(pe, x_in[t % 2], b * 64 + 16 * (t // 2 + 1))
                    if t >= 2:
                        wait(pe, "emb_h", b * TILES + t - 1)
                for k in range(2 * part, 2 * part + 2):
                    last = mm(spare(t)[:, 0:D], xt[:, t % 2, k, :], wp[:, k, :], start=(k == 0), stop=(k == KC - 1))
                if part == 2:
                    last.then_inc(S["emb_mm"], 1)

            def turn(b, j):
                hf, w = j // 4, j % 4
                wait(pe, "n_ready", b + 1)
                if j >= 2:
                    wait(pe, "tr_read", b * 8 + j - 1)
                src, c = (n, a)[w // 2], w % 2
                for t in range(4):
                    last = nc.tensor.transpose(spare(j)[:, t * P:(t + 1) * P],
                                               src[:, 4 * hf + t, c * P:(c + 1) * P], ident[:])
                last.then_inc(S["tr_mm"], 1)

            def project(b, g, j, c):
                hf, w = j // 2, j % 2
                if j >= 2 and c == 0:
                    wait(pe, "qk_lo", b * 8 + 4 * g + j - 1)
                last = mm(spare(j), wqk[:, c, w * D + g * P:w * D + (g + 1) * P],
                          nt[:, c, hf * HALF:(hf + 1) * HALF], start=(c == 0), stop=(c == DC - 1))
                if c == DC - 1:
                    last.then_inc(S["qk_mm"], 1)

            def score(b, k):
                g, i, hh = k // G_STEPS, (k % G_STEPS) // 4, k % 4
                if k % G_STEPS == 0:
                    wait(pe, stacked[g], (b * 24 + 24) * 16)
                if k >= SR:
                    wait(pe, "exp_done", b * STEPS + k - SR + 1)
                for j in range(2):
                    last = mm(ps[:, 2 * (k % SR) + j, :], stq[:, hh, i * P:(i + 1) * P],
                              stk[:, hh, j * 512:(j + 1) * 512], start=True, stop=True)
                last.then_inc(S["score_mm"], 1)

            def weigh(b, gi, j):
                i = gi % TILES
                if j == 0:
                    wait(pe, "vs_ready", b * 16 + gi + 1)
                    if i == 0:
                        wait(pe, "og_ready", b * 4 + 2 * (gi // TILES))
                for hh in range(4):
                    last = mm(ps[32 * hh:32 * hh + 32, O_BANK + j // 2, (j % 2) * D:(j % 2 + 1) * D], vs[:, gi % 2, hh, :],
                              pr[:, (4 * gi + hh) % PR, j * D:(j + 1) * D],
                              start=(i == 0 and j % 2 == 0), stop=(i == TILES - 1), skip_group_check=True)
                if j == 3:
                    last.then_inc(S["pv_mm"], 1)

            def values(b, pair):
                if pair == 0:
                    wait(pe, "qk_lo", b * 8 + 4)
                for j in (2 * pair, 2 * pair + 1):
                    if j >= 2:
                        wait(pe, "v_read", b * 4 + j - 1)
                    for t in range(2):
                        for c in range(DC):
                            last = mm(spare(j)[:, t * D:(t + 1) * D], nt[:, c, (2 * j + t) * P:(2 * j + t + 1) * P],
                                      wv[:, c, :], start=(c == 0), stop=(c == DC - 1), skip_group_check=True)
                    last.then_inc(S["v_mm"], 1)

            def gates(b, c2, hf, c):
                last = mm(spare(hf), wg[:, c, c2 * P:(c2 + 1) * P],
                          at[:, c, hf * HALF:(hf + 1) * HALF], start=(c == 0), stop=(c == DC - 1))
                if c == DC - 1:
                    last.then_inc(S["g_mm"], 1)

            def final(b):
                wait(pe, "og_ready", b * 4 + 4)
                for j in range(4):
                    if j >= 2:
                        wait(pe, "fin_h", b * 4 + j - 1)
                    elif isinstance(b, int) and b == IMAGES - 1:
                        wait(pe, "g_exp", b * 4 + 3 + j)
                    else:
                        wait(pe, "v_read", b * 4 + 7 + j)
                    for t in range(2):
                        for c in range(DC):
                            last = mm(spare(j)[:, t * D:(t + 1) * D], gate[:, c, (2 * j + t) * P:(2 * j + t + 1) * P],
                                      wfin[:, c, :], start=(c == 0), stop=(c == DC - 1), skip_group_check=True)
                    last.then_inc(S["fin_mm"], 1)

            def norm_turn(b, exps):
                wait(pe, "xn_ready", b + 1)
                for j in range(4):
                    hf, c = j // 2, j % 2
                    if j % 2 == 0:
                        wait(pe, "exp_done", exps - 1 + j // 2)
                    for t in range(4):
                        last = nc.tensor.transpose(ps[:, j, t * P:(t + 1) * P],
                                                   n[:, 4 * hf + t, c * P:(c + 1) * P], ident[:])
                    last.then_inc(S["xt_mm"], 1)

            def hidden(b, hf, k, bank):
                half = slice(hf * HALF, (hf + 1) * HALF)
                for c in range(DC):
                    w_high, w_low = wf1[:, 0, c, k * P:(k + 1) * P], wf1[:, 1, c, k * P:(k + 1) * P]
                    mm(spare(bank), w_high, nt_high[:, c, half], start=(c == 0), stop=False)
                    mm(spare(bank), w_high, nt_low[:, c, half], start=False, stop=False)
                    last = mm(spare(bank), w_low, nt_high[:, c, half], start=False, stop=(c == DC - 1))
                last.then_inc(S["ff_mm"], 1)

            def partial_logits(b, hf, bank):
                wait(pe, "ff_act", b * 16 + 8 * hf + 8)
                for k in range(HC):
                    cg = 32 * (k % 4)
                    last = mm(spare(bank)[cg:cg + 32, :], wr[:, k, :], ht[:, k, :], start=(k < 4), stop=(k >= 4))
                last.then_inc(S["lg_mm"], 1)

            def turn_logits(b, hf, bank):
                wait(pe, "lt_ready", b * 2 + hf + 1)
                for t in range(4):
                    last = mm(spare(bank)[:, t * EXPERTS:(t + 1) * EXPERTS], lt[:, t * P:(t + 1) * P], pick[:],
                              start=True, stop=True)
                last.then_inc(S["lg2_mm"], 1)

            def router(b):
                for k in range(HC):
                    if k == 0:
                        wait(pe, "xt_read", b * 4 + 4)
                    if k >= 2:
                        wait(pe, "ff_act", b * 16 + k - 1)
                    hidden(b, 0, k, k)
                partial_logits(b, 0, 0)
                hidden(b, 1, 0, 1)
                turn_logits(b, 0, 0)
                for k in range(1, HC):
                    if k == 2:
                        wait(pe, "lg_done", b * 2 + 1)
                    else:
                        wait(pe, "ff_act", b * 16 + 8 + (k - 1 if k > 2 else 1))
                    hidden(b, 1, k, 1 if k == 1 else k)

            def front_start(b):
                for t in range(TILES):
                    for part in range(3):
                        embed(b, t, part)
                wait(pe, "emb_h", b * TILES + TILES)
                for j in range(8):
                    turn(b, j)
                wait(pe, "tr_read", b * 8 + 8)
                for j in range(4):
                    for c in range(DC):
                        project(b, 0, j, c)

            pe.wait_ge(S["consts"], 16 * N_CONSTS)
            front_start(0)

            def image(b, par, before, after):
                values(b, 0)
                if before:
                    for j in range(4):
                        weigh(b - 1, 15, j)
                values(b, 1)
                if before:
                    final(b - 1)
                for j in range(2):
                    if before:
                        wait(pe, "fin_h", b * 4 - 1 + j)
                    else:
                        wait(pe, "v_read", b * 4 + 3 + j)
                    for c in range(DC):
                        gates(b, 0, j, c)
                for k in range(STEPS):
                    if k == G_STEPS:
                        if after:
                            wait(pe, "emb_h", (b + 1) * TILES + TILES)
                        else:
                            wait(pe, "qk_lo", b * 8 + 8)
                        if before:
                            norm_turn(b - 1, b * STEPS + G_STEPS)
                        for j in range(4):
                            weigh(b, 7, j)
                        if before:
                            router(b - 1)
                    score(b, k)
                    if before and k == G_STEPS + 1:
                        partial_logits(b - 1, 1, 0)
                    if before and k == G_STEPS + 2:
                        turn_logits(b - 1, 1, 1)
                    if k in QK1_AT:
                        j, c = QK1_AT[k]
                        if j < 2 and c == 0:
                            wait(pe, "g_exp", b * 4 + 1 + j)
                        project(b, 1, j, c)
                    if after and k in EMBED_AT:
                        t, part = EMBED_AT[k]
                        if t < 2 and part == 0:
                            wait(pe, "qk_lo", b * 8 + 7 + t)
                        embed(b + 1, t, part)
                    if k in GATE_AT:
                        hf, c = GATE_AT[k]
                        if before and hf == 0 and c == 0:
                            wait(pe, "lg_done", b * 2)
                        gates(b, 1, hf, c)
                    if after and k in TURN_AT:
                        if TURN_AT[k] < 2:
                            wait(pe, "g_exp", b * 4 + 3 + TURN_AT[k])
                        turn(b + 1, TURN_AT[k])
                    if after and k in QK0_AT:
                        j, c = QK0_AT[k]
                        if j == 0 and c == 0:
                            wait(pe, "tr_read", b * 8 + 16)
                        project(b + 1, 0, j, c)
                    for gi, j in WEIGH_AT[k]:
                        weigh(b, gi, j)

            over_images(pe, image)
            for j in range(4):
                weigh(IMAGES - 1, 15, j)
            final(IMAGES - 1)
            pe.wait_ge(S["fin_h"], IMAGES * 4)
            norm_turn(IMAGES - 1, IMAGES * STEPS)
            router(IMAGES - 1)
            partial_logits(IMAGES - 1, 1, 0)
            turn_logits(IMAGES - 1, 1, 1)

            pe.wait_ge(S["r_oh"], 1)
            oh_flat = oh[:].rearrange("p t e -> p (t e)")
            mm(ps[:, 0, :], up[:], oh_flat, start=True, stop=True)
            mm(ps[:, 1, :], ones[:].bitcast(F32), oh_flat, start=True, stop=True).then_inc(S["r_mm"], 1)

            def sort(j, first, last):
                for i in range(2):
                    wait(pe, "val_ready", j * 2 + i + 1)
                    for t in range(8):
                        done = mm(ps[:, 2, 0:2 * SLOTS], row_hot[:, i, t, :], slot_val[:, i, t],
                                  start=(first and i == 0 and t == 0), stop=(last and i == 1 and t == 7),
                                  skip_group_check=True)
                    done.then_inc(S["sort_mm"], 1)

            SORT_PAIRS = ALL_TILES // 16
            sort(0, True, False)
            with pe.Fori(1, SORT_PAIRS - 1) as j:
                sort(j, False, False)
            sort(SORT_PAIRS - 1, False, True)

            pe.wait_ge(S["slots_ready"], 1)

            def turn_group(g, i):
                wait(pe, xg_in[i], (g - i) * (FULL // 2) + FULL)
                for c in range(DC):
                    wait(pe, "gt_read", g * 2 + c - 1)
                    for t in range(GROUP):
                        last = nc.tensor.transpose(ps[:, c, t * P:(t + 1) * P],
                                                   xg[:, i, t, c * P:(c + 1) * P], ident[:])
                    last.then_inc(S["gt_mm"], 1)

            def group_hidden(g, i):
                wait(pe, "gt_read", g * 2 + 2)
                for k in range(HC):
                    wait(pe, "gf_act", g * 8 + k - 3)
                    for c in range(DC):
                        for part, (w_part, x_part) in enumerate(((0, 0), (0, 1), (1, 0))):
                            last = mm(ps[:, 2 + k % 4, 0:GROUP * P], wf1[:, w_part, c, k * P:(k + 1) * P],
                                      xgt[:, i, x_part, c, :], start=(c == 0 and part == 0),
                                      stop=(c == DC - 1 and part == 2))
                    last.then_inc(S["gf_mm"], 1)

            def group_rows(g, i):
                wait(pe, "hid_low", g * 8 + 8)
                for t in range(GROUP):
                    wait(pe, "y_ready", g * 2 + t - 1)
                    e = pe.value_load(slot_expert[0:1, bass.ds(g * GROUP + t, 1)], min_val=0, max_val=EXPERTS - 1)
                    o = ps[:, 6 + t, 0:D]
                    for k in range(HC):
                        for h_part, w_part in ((0, 0), (0, 1), (1, 0)):
                            mm(o, hg[:, i, h_part, k, t * P:(t + 1) * P], wd[:, w_part, bass.ds(e, 1), k, :],
                               start=(k == 0 and h_part == w_part), stop=False)
                    mm(o, ones[0:2, :], bd[:, bass.ds(e, 1), :], start=False, stop=True).then_inc(S["y_mm"], 1)

            def stage(g, i):
                group_hidden(g, i)
                turn_group(g + 1, 1 - i)
                group_rows(g - 1, 1 - i)

            turn_group(0, 0)
            group_hidden(0, 0)
            turn_group(1, 1)
            pe.wait_ge(S["wd_low"], WD_PIECES)
            pe.wait_ge(S["bd_in"], 16 * 2 * EXPERTS)
            stage(1, 1)
            with pe.Fori(1, SORT_GROUPS // 2 - 1) as j:
                stage(j * 2, 0)
                stage(j * 2 + 1, 1)
            stage(SORT_GROUPS - 2, 0)
            group_hidden(SORT_GROUPS - 1, 1)
            group_rows(SORT_GROUPS - 2, 0)
            group_rows(SORT_GROUPS - 1, 1)

        @block.scalar
        def _(act):
            actv = nc.scalar.activation

            def spare(j):
                return ps[:, SPARE + j % 2, :]

            for j in range(4):
                act.wait_ge(S["pos_mm"], j + 1)
                actv(posr[:, j // 2, (j % 2) * HALF:(j % 2 + 1) * HALF], ps[:, j, :], ACT.Relu).then_inc(S["pos_relu"], 1)
            for j in range(4):
                act.wait_ge(S["pos_mm2"], 2 * j + 2)
                actv(posb[:, 2 * j:2 * j + 2, :].rearrange("p t d -> p (t d)"), ps[:, 4 + j, :], ACT.Identity
                     ).then_inc(S["pos_done"], 1)

            act.wait_ge(S["consts"], 16 * N_CONSTS)
            actv(wf1[:, 0], wf1_in, ACT.Identity).then_inc(S["wf1_high"], 1)

            def turned(b, j):
                hf, w = j // 4, j % 4
                wait(act, "tr_mm", b * 8 + j + 1)
                if w < 2:
                    actv(nt[:, w, hf * HALF:(hf + 1) * HALF], spare(j), ACT.Identity,
                         bias=beta[:, w:w + 1], scale=gamma[:, w:w + 1]).then_inc(S["tr_read"], 1)
                else:
                    actv(at[:, w - 2, hf * HALF:(hf + 1) * HALF], spare(j), ACT.Identity).then_inc(S["tr_read"], 1)

            def high(b, g, j):
                hf, w = j // 2, j % 2
                wait(act, "qk_mm", b * 8 + 4 * g + j + 1)
                if j == 0:
                    if g == 0:
                        wait(act, stacked[1], b * 24 * 16)
                    else:
                        wait(act, stacked[0], (b * 24 + 24) * 16)
                actv(qk[:, w, 0, hf * HALF:(hf + 1) * HALF], spare(j), ACT.Identity,
                     scale=(SCALE if w == 0 else 1.0)).then_inc(S["qk_hi"], 1)

            def gated_exp(b, c, hf):
                wait(act, "g_mm", b * 4 + 2 * c + hf + 1)
                actv(gate[:, c, hf * HALF:(hf + 1) * HALF], spare(hf), ACT.Exp,
                     bias=nbgate[:, c:c + 1], scale=-1.0).then_inc(S["g_exp"], 1)

            def router(b):
                for j in range(4):
                    wait(act, "xt_mm", b * 4 + j + 1)
                    actv(nt_high[:, j % 2, (j // 2) * HALF:(j // 2 + 1) * HALF], ps[:, j, :], ACT.Identity).then_inc(S["xt_high"], 1)
                for hf in range(2):
                    for k in range(HC):
                        bank = 1 if hf == 1 and k == 0 else k
                        wait(act, "ff_mm", b * 16 + 8 * hf + k + 1)
                        if hf == 1:
                            wait(act, "lg_mm", b * 2 + 1)
                        actv(ht[:, k, :], spare(bank), ACT.Gelu, bias=bf1[:, k:k + 1]).then_inc(S["ff_act"], 1)

            for j in range(8):
                turned(0, j)
            for j in range(4):
                high(0, 0, j)

            def image(b, par, before, after):
                for j in range(4):
                    wait(act, "v_mm", b * 4 + j + 1)
                    wait(act, "vs_ready", b * 16)
                    actv(v[:, 2 * j:2 * j + 2, :].rearrange("p t d -> p (t d)"), spare(j), ACT.Identity
                         ).then_inc(S["v_read"], 1)
                if before:
                    wait(act, "fin_mm", b * 4)
                for hf in range(2):
                    gated_exp(b, 0, hf)
                for k in range(STEPS):
                    if k == G_STEPS and before:
                        router(b - 1)
                    wait(act, "max_done", b * STEPS + k + 1)
                    if before and k == G_STEPS + 2:
                        wait(act, "lg2_mm", b * 2)
                    if before and k == G_STEPS + 4:
                        wait(act, "lg_mm", b * 2)
                    if k >= PR:
                        wait(act, "pv_mm", b * 16 + (k - PR) // 4 + 1)
                    actv(pr[:, k % PR, :], ps[:, 2 * (k % SR):2 * (k % SR) + 2, :].rearrange("p a n -> p (a n)"),
                         ACT.Exp, bias=nmax[:, k % 16:k % 16 + 1], accum_out=rsum[:, k % 16:k % 16 + 1]
                         ).then_inc(S["exp_done"], 1)
                    if after and k in TURN_AT:
                        turned(b + 1, TURN_AT[k])
                    if k in GATE_AT and GATE_AT[k][1] == 1:
                        gated_exp(b, 1, GATE_AT[k][0])
                    if k in QK1_AT and QK1_AT[k][1] == 1:
                        high(b, 1, QK1_AT[k][0])
                    if after and k in QK0_AT and QK0_AT[k][1] == 1:
                        high(b + 1, 0, QK0_AT[k][0])

            over_images(act, image)
            router(IMAGES - 1)
            act.wait_ge(S["r_exp"], 1)
            actv(ee[:], ee[:], ACT.Exp).then_inc(S["r_exp"], 1)

            act.wait_ge(S["bd_raw_in"], 16)
            actv(bd_parts[:, 0], bd_raw[:], ACT.Identity).then_inc(S["bd_high"], 1)

            def high_down(j):
                for i in range(WD_BUFFERS):
                    wait(act, wd_in[i], j * 16 + 16)
                    actv(wd_piece(0, j * WD_BUFFERS + i), wd_raw[:, i], ACT.Identity).then_inc(S["wd_high"], 1)

            over_pairs(act, WD_PIECES // WD_BUFFERS, high_down)

            def group_hidden(g, i):
                for c in range(DC):
                    wait(act, "gt_mm", g * 2 + c + 1)
                    actv(xgt[:, i, 0, c, :], ps[:, c, 0:GROUP * P], ACT.Identity).then_inc(S["gt_high"], 1)
                for k in range(HC):
                    wait(act, "gf_mm", g * 8 + k + 1)
                    wait(act, "hid_low", g * 8 + k - 1)
                    actv(hraw[:, k % 2, :], ps[:, 2 + k % 4, 0:GROUP * P], ACT.Gelu, bias=bf1[:, k:k + 1]
                         ).then_inc(S["gf_act"], 1)

            over_groups(act, group_hidden)

        @block.vector
        def _(dve):
            V = nc.vector

            def spare(j):
                return ps[:, SPARE + j % 2, :]

            V.memset(ones[:].bitcast(F32), 1.0).then_inc(S["setup"], 1)
            dve.wait_ge(S["consts"], 16 * N_CONSTS)
            V.tensor_scalar(nbgate[:], bgate, -1.0, None, ALU.mult).then_inc(S["setup"], 1)
            dve.wait_ge(S["setup"], 2)
            dve.wait_ge(S["wf1_high"], 1)
            V.tensor_tensor(wf1[:, 1], wf1_in, wf1[:, 0].bitcast(F32), ALU.subtract
                            ).then_inc(S["setup"], 1)

            def stats(src, b, ln):
                for t in range(TILES):
                    last = V.bn_stats(bst[:, ln - 1, t, :], src[:, t, :])
                last.then_inc(S[f"stats{ln}"], 1)
                hold(dve, f"stats{ln}", b + 1)
                for t in range(TILES):
                    last = V.bn_aggr(mv[:, ln - 1, t, :], bst[:, ln - 1, t, :])
                last.then_inc(S[f"var{ln}"], 1)

            def normalise(dst, src, b, ln, done):
                hold(dve, f"rstd{ln}", b + 1)
                for t in range(TILES):
                    last = V.tensor_scalar(dst[:, t, :], src[:, t, :], mv[:, ln - 1, t, 0:1],
                                           rstd[:, ln - 1, t:t + 1], ALU.subtract, ALU.mult)
                last.then_inc(S[done], 1)

            def embedded(b, par, t):
                wait(dve, "emb_mm", b * TILES + t + 1)
                if t == 0:
                    wait(dve, "h_out", b * 16 - 16)
                V.tensor_tensor(hres[:, par, t, :], spare(t)[:, 0:D], posb[:, t, :], ALU.add).then_inc(S["emb_h"], 1)

            def norm_1(b, par):
                wait(dve, "emb_h", b * TILES + TILES)
                stats(hres[:, par], b, 1)
                normalise(a, hres[:, par], b, 1, "a_ready")

            def stats_2(b):
                wait(dve, "a_ready", b + 1)
                stats(a, b, 2)

            def norm_2(b, before):
                if before:
                    wait(dve, "xn_out", b * 16 - 16)
                    wait(dve, "xt_mm", b * 4 - 4)
                normalise(n, a, b, 2, "n_ready")

            def low(b, g, j):
                hf, w = j // 2, j % 2
                wait(dve, "qk_hi", b * 8 + 4 * g + j + 1)
                V.scalar_tensor_tensor(
                    qk[:, w, 1, hf * HALF:(hf + 1) * HALF], spare(j), SCALE if w == 0 else 1.0,
                    qk[:, w, 0, hf * HALF:(hf + 1) * HALF].bitcast(F32), ALU.mult, ALU.subtract
                ).then_inc(S["qk_lo"], 1)

            def scale_v(b, gi):
                g, i = gi // TILES, gi % TILES
                col = (4 * gi) % 16
                wait(dve, "exp_done", b * STEPS + 4 * gi + 4)
                V.reciprocal(rinv[:, gi % 2, :], rsum[:, col:col + 4]).then_inc(S["rinv_done"], 1)
                wait(dve, "rinv_done", b * 16 + gi + 1)
                wait(dve, "pv_mm", b * 16 + gi - 1)
                V.tensor_tensor(vs[:, gi % 2], v[:, i, g * P:(g + 1) * P].rearrange("p (a d) -> p a d", a=4),
                                rinv[:, gi % 2, :, None].broadcast_to([P, 4, HD]), ALU.mult).then_inc(S["vs_ready"], 1)

            def invert(b, c, q):
                if q % 4 == 0:
                    wait(dve, "g_one", b * 4 + 2 * c + q // 4 + 1)
                piece = gate[:, c, q * P:(q + 1) * P]
                V.reciprocal(piece, piece).then_inc(S["g_ready"], 1)

            def gated(b, g):
                wait(dve, "pv_mm", b * 16 + 8 * (g + 1))
                wait(dve, "g_ready", b * 16 + 8 * (g + 1))
                for j in range(2):
                    piece = gate[:, g, j * 512:(j + 1) * 512]
                    V.tensor_tensor(piece, ps[:, O_BANK + j, :], piece, ALU.mult).then_inc(S["og_ready"], 1)

            def added(b, par):
                h = hres[:, par].rearrange("p t d -> p (t d)")
                wait(dve, "ha_ready", b + 1)
                for j in range(4):
                    wait(dve, "fin_mm", b * 4 + j + 1)
                    V.tensor_tensor(h[:, j * 512:(j + 1) * 512], h[:, j * 512:(j + 1) * 512], spare(j), ALU.add
                                    ).then_inc(S["fin_h"], 1)

            def stats_3(b, par):
                wait(dve, "fin_h", b * 4 + 4)
                stats(hres[:, par], b, 3)

            def norm_3(b, par, t):
                if t == 0:
                    wait(dve, "tr_mm", b * 8 + 16 if not isinstance(b, int) or b < IMAGES - 1 else b * 8 + 8)
                    hold(dve, "rstd3", b + 1)
                last = V.tensor_scalar(n[:, t, :], hres[:, par, t, :], mv[:, 2, t, 0:1], rstd[:, 2, t:t + 1],
                                       ALU.subtract, ALU.mult)
                if t == TILES - 1:
                    last.then_inc(S["xn_ready"], 1)

            def low_norm(b):
                for j in range(4):
                    piece = slice((j // 2) * HALF, (j // 2 + 1) * HALF)
                    wait(dve, "xt_high", b * 4 + j + 1)
                    V.tensor_tensor(nt_low[:, j % 2, piece], ps[:, j, :], nt_high[:, j % 2, piece].bitcast(F32), ALU.subtract
                                    ).then_inc(S["xt_read"], 1)

            def logit_sums(b, hf):
                wait(dve, "lg_mm", b * 2 + hf + 1)
                if hf == 1:
                    wait(dve, "lg2_mm", b * 2 + 1)
                V.tensor_copy(lt, spare(0)).then_inc(S["lt_ready"], 1)

            def keep_logits(b, hf):
                wait(dve, "lg2_mm", b * 2 + hf + 1)
                V.tensor_copy(logits[:, bass.ds(b * TILES + 4 * hf, 4), :],
                              spare(hf)[:, 0:4 * EXPERTS].rearrange("p (t e) -> p t e", e=EXPERTS)
                              ).then_inc(S["lg_done"], 1)

            for t in range(TILES):
                embedded(0, 0, t)
            norm_1(0, 0)
            stats_2(0)
            norm_2(0, False)
            for j in range(4):
                low(0, 0, j)

            def image(b, par, before, after):
                if before:
                    scale_v(b - 1, 15)
                    gated(b - 1, 1)
                    added(b - 1, 1 - par)
                    stats_3(b - 1, 1 - par)
                for k in range(STEPS):
                    if k == G_STEPS:
                        scale_v(b, 7)
                        if before:
                            low_norm(b - 1)
                        if after:
                            norm_1(b + 1, 1 - par)
                            stats_2(b + 1)
                        if before:
                            logit_sums(b - 1, 0)
                            keep_logits(b - 1, 0)
                        if after:
                            norm_2(b + 1, before)
                        gated(b, 0)
                    wait(dve, "score_mm", b * STEPS + k + 1)
                    V.reduce_max(nmax[:, k % 16:k % 16 + 1],
                                 ps[:, 2 * (k % SR):2 * (k % SR) + 2, :].rearrange("p a n -> p (a n)"),
                                 AX_X, negate=True).then_inc(S["max_done"], 1)
                    if before and k == G_STEPS + 1:
                        logit_sums(b - 1, 1)
                    if before and k == G_STEPS + 2:
                        keep_logits(b - 1, 1)
                    if k in SCALE_AT:
                        scale_v(b, SCALE_AT[k])
                    if before and k in NORM_AT:
                        norm_3(b - 1, 1 - par, NORM_AT[k])
                    if k in INVERT_AT:
                        invert(b, *INVERT_AT[k])
                    if k in LOW1_AT:
                        low(b, 1, LOW1_AT[k])
                    if after and k in EMBED_AT and EMBED_AT[k][1] == 2:
                        embedded(b + 1, 1 - par, EMBED_AT[k][0])
                    if after and k in LOW0_AT:
                        low(b + 1, 0, LOW0_AT[k])

            over_images(dve, image)
            last_b, last_par = IMAGES - 1, (IMAGES - 1) % 2
            scale_v(last_b, 15)
            gated(last_b, 1)
            added(last_b, last_par)
            stats_3(last_b, last_par)
            dve.wait_ge(S["xn_out"], 16 * last_b)
            for t in range(TILES):
                norm_3(last_b, last_par, t)
            low_norm(last_b)
            for hf in range(2):
                logit_sums(last_b, hf)
                keep_logits(last_b, hf)

            links = [0]

            def link(ins):
                links[0] += 1
                ins.then_inc(S["chain"], 1)
                dve.wait_ge(S["chain"], links[0])

            wide = [P, ALL_TILES, EXPERTS]
            dve.wait_ge(S["lg_done"], 2 * IMAGES)
            dve.wait_ge(S["h_out"], 16 * IMAGES)
            dve.wait_ge(S["xn_out"], 16 * IMAGES)
            link(V.tensor_tensor(logits[:], logits[:], brt[:, None, :].broadcast_to(wide), ALU.add))
            link(V.reduce_max(red[:, 0, :], logits[:], AX_X))
            V.tensor_tensor(ee[:], logits[:], red[:, 0, :, None].broadcast_to(wide), ALU.subtract).then_inc(S["r_exp"], 1)
            link(V.memset(onesf[:], 1.0))
            dve.wait_ge(S["r_exp"], 2)
            link(V.reduce_max(red[:, 1, :], ee[:], AX_X))
            link(V.tensor_tensor(oh[:], ee[:], red[:, 1, :, None].broadcast_to(wide), ALU.is_ge))
            link(V.tensor_tensor(oh[:], oh[:], rnk[:, None, :].broadcast_to(wide), ALU.mult))
            link(V.reduce_max(red[:, 3, :], oh[:], AX_X))
            V.tensor_tensor(oh[:], oh[:], red[:, 3, :, None].broadcast_to(wide), ALU.is_equal).then_inc(S["r_oh"], 1)
            link(V.reduce_sum(red[:, 2, :], ee[:], AX_X))
            link(V.reciprocal(red[:, 2, :], red[:, 2, :]))
            link(V.tensor_tensor(prob[:], red[:, 1, :], red[:, 2, :], ALU.mult))
            dve.wait_ge(S["r_mm"], 1)
            link(V.tensor_copy(tot[:].rearrange("p t e -> p (t e)"), ps[:, 1, :]))
            for e in range(EXPERTS):
                V.tensor_tensor_scan(run[:, :, e], onesf[:], tot[:, :, e], 0.0, ALU.mult, ALU.add)
            link(V.memset(slot_f[:], 0.0))
            link(V.tensor_scalar(cnt_i[:, 0, :], run[:, ALL_TILES - 1, :], float(P - 1), None, ALU.add))
            link(V.tensor_scalar(cnt_i[:, 1, :], cnt_i[:, 0, :], 7, 7, ALU.arith_shift_right, ALU.logical_shift_left))
            link(V.tensor_copy(cnt[:, 0, :], cnt_i[:, 1, :]))
            link(V.tensor_tensor_scan(cnt[:, 1, :], onesf[:, 0:EXPERTS], cnt[:, 0, :], 0.0, ALU.mult, ALU.add))
            link(V.tensor_tensor(cnt[:, 2, :], cnt[:, 1, :], cnt[:, 0, :], ALU.subtract))
            link(V.tensor_tensor(run[:], run[:], tot[:], ALU.subtract))
            link(V.tensor_tensor(run[:].rearrange("p t e -> p (t e)"), run[:].rearrange("p t e -> p (t e)"), ps[:, 0, :], ALU.add))
            link(V.tensor_tensor(run[:], run[:], cnt[:, 2, None, :].broadcast_to(wide), ALU.add))
            link(V.tensor_tensor(run[:], run[:], oh[:], ALU.mult))
            link(V.reduce_sum(place_f[:], run[:], AX_X))
            link(V.tensor_copy(place_i[:], place_f[:]))
            link(V.tensor_scalar(low_i[:], place_i[:], P - 1, None, ALU.bitwise_and))
            link(V.tensor_copy(low_f[:], low_i[:]))
            link(V.tensor_tensor(high_f[:], place_f[:], low_f[:], ALU.subtract))

            def select(j):
                for i in range(2):
                    tiles = bass.ds(j * 16 + 8 * i, 8)

                    def each(src, width):
                        return src[:, tiles, None].broadcast_to([P, 8, width])

                    wait(dve, "sort_mm", j * 2 + i - 1)
                    V.tensor_tensor(slot_val[:, i, :, 1, :], sst[:, None, :].broadcast_to([P, 8, SLOTS]),
                                    each(high_f, SLOTS), ALU.is_equal).then_inc(S["hot_ready"], 1)
                    V.tensor_tensor(row_hot[:, i], col[:, None, :].broadcast_to([P, 8, P]),
                                    each(low_f, P), ALU.is_equal)
                    wait(dve, "hot_ready", j * 2 + i + 1)
                    V.tensor_tensor(slot_val[:, i, :, 0, :], slot_val[:, i, :, 1, :], each(tid, SLOTS), ALU.mult)
                    V.tensor_tensor(slot_val[:, i, :, 1, :], slot_val[:, i, :, 1, :], each(prob, SLOTS), ALU.mult
                                    ).then_inc(S["val_ready"], 1)

            over_pairs(dve, ALL_TILES // 16, select)
            for e in range(EXPERTS):
                link(V.scalar_tensor_tensor(slot_f[:, (e + 1) % 2, :], sst[:], cnt[:, 1, e:e + 1], slot_f[:, e % 2, :],
                                            ALU.is_ge, ALU.add))
            V.tensor_scalar(slot_expert[:], slot_f[:, EXPERTS % 2, :], float(EXPERTS - 1), None, ALU.min).then_inc(S["slots_ready"], 1)
            dve.wait_ge(S["sort_mm"], ALL_TILES // 8)
            V.tensor_scalar(slot_to[:], ps[:, 2, 0:SLOTS], float(ALL_TILES * P), None, ALU.add)
            V.tensor_scalar(slot_from[:], ps[:, 2, 0:SLOTS], float(ALL_TILES * P), float(ALL_TILES * P - 1),
                            ALU.add, ALU.min)
            V.tensor_copy(slot_prob[:], ps[:, 2, SLOTS:2 * SLOTS]).then_inc(S["slots_in"], 1)

            def turned_rows(g, i):
                for c in range(DC):
                    wait(dve, "gt_high", g * 2 + c + 1)
                    V.tensor_tensor(xgt[:, i, 1, c, :], ps[:, c, 0:GROUP * P], xgt[:, i, 0, c, :].bitcast(F32), ALU.subtract
                                    ).then_inc(S["gt_read"], 1)

            def split_hidden(g, i):
                wait(dve, "y_mm", g * 2 - 2)
                for k in range(HC):
                    high_part, low_part = hg[:, i, 0, k, :], hg[:, i, 1, k, :]
                    wait(dve, "gf_act", g * 8 + k + 1)
                    V.tensor_copy(high_part, hraw[:, k % 2, :]).then_inc(S["hid_high"], 1)
                    wait(dve, "hid_high", g * 8 + k + 1)
                    V.tensor_tensor(low_part, hraw[:, k % 2, :], high_part.bitcast(F32), ALU.subtract
                                    ).then_inc(S["hid_low"], 1)

            def expert_rows(g, i):
                V.tensor_copy(pcol[:, i], slot_prob[:, bass.ds(g * GROUP, GROUP)]).then_inc(S["pcol_ready"], 1)
                wait(dve, "pcol_ready", g + 1)
                wait(dve, hr_in[i], (g - i) * (FULL // 2) + FULL)
                for t in range(GROUP):
                    wait(dve, "y_mm", g * 2 + t + 1)
                    V.scalar_tensor_tensor(hr[:, i, t, :], ps[:, 6 + t, 0:D], pcol[:, i, t:t + 1], hr[:, i, t, :],
                                           ALU.mult, ALU.add).then_inc(S["y_ready"], 1)

            def stage(g, i):
                split_hidden(g, i)
                turned_rows(g + 1, 1 - i)
                expert_rows(g - 1, 1 - i)

            turned_rows(0, 0)
            dve.wait_ge(S["bd_in"], 16 * 2 * EXPERTS)
            split_hidden(0, 0)
            turned_rows(1, 1)
            stage(1, 1)
            with dve.Fori(1, SORT_GROUPS // 2 - 1) as j:
                stage(j * 2, 0)
                stage(j * 2 + 1, 1)
            stage(SORT_GROUPS - 2, 0)
            split_hidden(SORT_GROUPS - 1, 1)
            expert_rows(SORT_GROUPS - 2, 0)
            expert_rows(SORT_GROUPS - 1, 1)


def kernel(**inputs):
    import numpy as np
    import concourse.bacc as bacc
    from concourse.bass_utils import run_bass_kernel_spmd

    c = np.ascontiguousarray

    def chunked(w):
        return c(w.reshape(-1, P, w.shape[-1]).transpose(1, 0, 2))

    a = {k: np.asarray(v) for k, v in inputs.items()}
    x = a["x"].reshape(IMAGES, 3, 32, 16, 32, 16).transpose(0, 1, 3, 5, 2, 4).reshape(IMAGES, KC, P, TILES, P)
    x = c(x.transpose(0, 3, 2, 1, 4))
    f32 = np.float32
    grid = np.arange(32, dtype=f32) / f32(31)
    pos_in = np.stack([np.repeat(grid, 32), np.tile(grid, 32), np.ones(TOKENS, f32)])
    w_qkv = a["L0_attn_W_qkv"].T
    router = np.concatenate([a["L0_ffn_Wg"], np.zeros((HID, 32 - EXPERTS), f32)], 1)
    pick = np.tile(np.concatenate([np.eye(EXPERTS, dtype=f32), np.zeros((32 - EXPERTS, EXPERTS), f32)]), (4, 1))
    rank = np.tile((EXPERTS - np.arange(EXPERTS, dtype=f32)), (P, 1))
    tid = (np.arange(ALL_TILES)[None, :] * P + np.arange(P)[:, None] - ALL_TILES * P).astype(f32)
    arrays = {
        "x_in": x,
        "w_patch": chunked(a["L0_tok_Wp"]),
        "pos_in": c(pos_in),
        "pos_w1": c(np.concatenate([a["L0_tok_W1"], a["L0_tok_b1"][None]], 0)),
        "pos_w2": chunked(a["L0_tok_W2"]),
        "pos_bias": c(np.stack([a["L0_tok_b2"], a["L0_tok_bp"]])),
        "ln_gamma": c(a["L0_attn_ln_gamma"].reshape(DC, P).T),
        "ln_beta": c(a["L0_attn_ln_beta"].reshape(DC, P).T),
        "w_qk": chunked(w_qkv[:, :2 * D]),
        "w_v": chunked(w_qkv[:, 2 * D:]),
        "w_gate": chunked(a["L0_attn_W_gate"].T),
        "b_gate": c(a["L0_attn_b_gate"].reshape(DC, P).T),
        "w_final": chunked(a["L0_attn_W_final"].T),
        "b_final": c(np.tile(a["L0_attn_b_final"], (P, 1))),
        "w_ffn1": chunked(a["L0_ffn_W1"]),
        "b_ffn1": c(a["L0_ffn_b1"].reshape(HC, P).T),
        "w_router": chunked(router),
        "b_router": c(np.tile(a["L0_ffn_bg"], (P, 1))),
        "w_down": c(a["L0_ffn_Wd"].reshape(WD_PIECES, HC // 2, P, D).transpose(0, 2, 1, 3)),
        "b_down": c(a["L0_ffn_bd"]),
        "identity": np.eye(P, dtype=f32),
        "pick_in": pick,
        "upper": np.triu(np.ones((P, P), f32), 1),
        "rank": c(rank),
        "slot_start": c(np.tile(np.arange(SLOTS, dtype=f32) * P, (P, 1))),
        "column": c(np.tile(np.arange(P, dtype=f32), (P, 1))),
        "token_id": c(tid),
    }
    nc = bacc.Bacc("TRN2", target_bir_lowering=False, num_devices=1)
    aps = [nc.dram_tensor(k, v.shape, mybir.dt.from_np(v.dtype), kind="ExternalInput").ap() for k, v in arrays.items()]
    aps.append(nc.dram_tensor("out", (IMAGES, TOKENS, D), F32, kind="ExternalOutput").ap())
    vit_layer_kernel(nc, *aps)
    r = run_bass_kernel_spmd(nc, [arrays], core_ids=[0])
    return r.results[0]["out"]
```
